# Optimizing a Trainium2 kernel written in Bass

```python
import numpy as np
import jax
import jax.numpy as jnp

def _softmax(x, axis=-1):
    return jax.nn.softmax(x, axis=axis)

def _gelu(x):
    return jax.nn.gelu(x, approximate=True)

def _silu(x):
    return jax.nn.silu(x)

def _sigmoid(x):
    return jax.nn.sigmoid(x)

def _layernorm(x, axis=-1, eps=1e-05):
    m = jnp.mean(x, axis=axis, keepdims=True)
    v = jnp.var(x, axis=axis, keepdims=True)
    return (x - m) / jnp.sqrt(v + eps)

def _scatter_add(tgt, idx, src, axis=0):
    return tgt.at[idx].add(src)

def _segment_sum(src, seg, n):
    return jax.ops.segment_sum(src, seg, n)
kernel_name = 'mk_adj_seq_d2_adj_r2_aeff53'

def setup_inputs(seed: int=0):
    np.random.seed(seed)
    _w = jnp.asarray

    def _rec_inputs():
        import jax
        import jax.numpy as jnp
        _gk = jax.random.key(seed)
        x = -0.0002928 + 1 * jax.random.normal(jax.random.fold_in(_gk, 1), (64, 128, 256), jnp.float32)
        _w = (1.0 + jnp.arange(128, dtype=jnp.float32)) ** (-0.5)
        _w = _w / _w.mean()
        _pij = jnp.clip(0.125 * _w[:, None] * _w[None, :], 0.0, 1.0)
        _a = jax.random.uniform(jax.random.fold_in(_gk, 2), (64, 128, 128)) < _pij
        _a = jnp.logical_or(_a, jnp.eye(128, dtype=bool))
        adj = _a.astype(jnp.int32)
        return (x, adj)
    x, adj = _rec_inputs()

    def _L0_gnn_setup():
        import jax, jax.numpy as jnp
        import numpy as np
        B, N, D, H = (4, 1024, 256, 8)
        HD = D // H
        EPS = 1e-05
        key = jax.random.key(seed)
        ks = jax.random.split(key, 12)
        x = jax.random.normal(ks[0], (B, N, D), dtype=jnp.float32)
        adj = jax.random.randint(ks[1], (B, N, N), 0, 2, dtype=jnp.int32)
        adj = jnp.maximum(adj, jnp.eye(N, dtype=jnp.int32)[None, :, :])
        s = 1.0 / np.sqrt(D)
        Wq = jax.random.uniform(ks[2], (D, D), jnp.float32, -s, s)
        bq = jnp.zeros((D,), jnp.float32)
        Wk = jax.random.uniform(ks[3], (D, D), jnp.float32, -s, s)
        bk = jnp.zeros((D,), jnp.float32)
        Wv = jax.random.uniform(ks[4], (D, D), jnp.float32, -s, s)
        bv = jnp.zeros((D,), jnp.float32)
        Wo = jax.random.uniform(ks[5], (D, D), jnp.float32, -s, s)
        bo = jnp.zeros((D,), jnp.float32)
        gamma = jnp.ones((D,), jnp.float32)
        beta = jnp.zeros((D,), jnp.float32)
        return {'x': x, 'adj': adj, 'Wq': Wq, 'bq': bq, 'Wk': Wk, 'bk': bk, 'Wv': Wv, 'bv': bv, 'Wo': Wo, 'bo': bo, 'gamma': gamma, 'beta': beta}
    _L0_gnn_all = _L0_gnn_setup()
    _L0_gnn_in = {k: v for k, v in _L0_gnn_all.items() if k in ('Wq', 'bq', 'Wk', 'bk', 'Wv', 'bv', 'Wo', 'bo', 'gamma', 'beta')}
    del _L0_gnn_all

    def _L1_gnn_setup():
        import jax, jax.numpy as jnp
        import numpy as np
        HIDDEN = 256
        NHEADS = 8
        ALPHA = 0.1
        NUM_HOP = 4
        MASK_VAL = -16384.0
        LN_EPS = 1e-05
        key = jax.random.key(seed)
        ks = jax.random.split(key, 10)
        B, N, H = (8, 512, HIDDEN)
        s = 1.0 / np.sqrt(H)
        x = jax.random.normal(ks[0], (B, N, H), dtype=jnp.float32)
        adj = jax.random.randint(ks[1], (B, N, N), 0, 2, dtype=jnp.int32)
        Wq = jax.random.uniform(ks[2], (H, H), jnp.float32, -s, s)
        bq = jax.random.uniform(ks[3], (H,), jnp.float32, -s, s)
        Wk = jax.random.uniform(ks[4], (H, H), jnp.float32, -s, s)
        bk = jax.random.uniform(ks[5], (H,), jnp.float32, -s, s)
        Wv = jax.random.uniform(ks[6], (H, H), jnp.float32, -s, s)
        bv = jax.random.uniform(ks[7], (H,), jnp.float32, -s, s)
        gamma = jnp.ones((H,), jnp.float32)
        beta = jnp.zeros((H,), jnp.float32)
        return {'x': x, 'adj': adj, 'Wq': Wq, 'bq': bq, 'Wk': Wk, 'bk': bk, 'Wv': Wv, 'bv': bv, 'gamma': gamma, 'beta': beta}
    _L1_gnn_all = _L1_gnn_setup()
    _L1_gnn_in = {k: v for k, v in _L1_gnn_all.items() if k in ('Wq', 'bq', 'Wk', 'bk', 'Wv', 'bv', 'gamma', 'beta')}
    del _L1_gnn_all
    return {'x': x, 'adj': adj, 'L0_gnn_Wq': _L0_gnn_in['Wq'], 'L0_gnn_bq': _L0_gnn_in['bq'], 'L0_gnn_Wk': _L0_gnn_in['Wk'], 'L0_gnn_bk': _L0_gnn_in['bk'], 'L0_gnn_Wv': _L0_gnn_in['Wv'], 'L0_gnn_bv': _L0_gnn_in['bv'], 'L0_gnn_Wo': _L0_gnn_in['Wo'], 'L0_gnn_bo': _L0_gnn_in['bo'], 'L0_gnn_gamma': _L0_gnn_in['gamma'], 'L0_gnn_beta': _L0_gnn_in['beta'], 'L1_gnn_Wq': _L1_gnn_in['Wq'], 'L1_gnn_bq': _L1_gnn_in['bq'], 'L1_gnn_Wk': _L1_gnn_in['Wk'], 'L1_gnn_bk': _L1_gnn_in['bk'], 'L1_gnn_Wv': _L1_gnn_in['Wv'], 'L1_gnn_bv': _L1_gnn_in['bv'], 'L1_gnn_gamma': _L1_gnn_in['gamma'], 'L1_gnn_beta': _L1_gnn_in['beta']}

def reference(x, adj, L0_gnn_Wq, L0_gnn_bq, L0_gnn_Wk, L0_gnn_bk, L0_gnn_Wv, L0_gnn_bv, L0_gnn_Wo, L0_gnn_bo, L0_gnn_gamma, L0_gnn_beta, L1_gnn_Wq, L1_gnn_bq, L1_gnn_Wk, L1_gnn_bk, L1_gnn_Wv, L1_gnn_bv, L1_gnn_gamma, L1_gnn_beta):
    import jax
    import jax.numpy as jnp

    def _L0_gnn_ref(x, adj, Wq, bq, Wk, bk, Wv, bv, Wo, bo, gamma, beta):
        import jax, jax.numpy as jnp
        import numpy as np
        B, N, D, H = (4, 1024, 256, 8)
        HD = D // H
        EPS = 1e-05
        b, n, d = x.shape
        scale = 1.0 / np.sqrt(HD).astype(np.float32)
        q = (x @ Wq + bq).reshape(b, n, H, HD)
        k = (x @ Wk + bk).reshape(b, n, H, HD)
        v = (x @ Wv + bv).reshape(b, n, H, HD)
        scores = jnp.einsum('bnhd,bmhd->bhnm', q, k) * scale
        mask = (adj == 0)[:, None, :, :]
        scores = jnp.where(mask, jnp.float32(-jnp.inf), scores)
        attn = jax.nn.softmax(scores, axis=-1)
        h = jnp.einsum('bhnm,bmhd->bnhd', attn, v).reshape(b, n, d)
        h = h @ Wo + bo
        y = h + x
        mu = jnp.mean(y, axis=-1, keepdims=True)
        var = jnp.mean(jnp.square(y - mu), axis=-1, keepdims=True)
        return (y - mu) * jax.lax.rsqrt(var + EPS) * gamma + beta

    def _L1_gnn_ref(x, adj, Wq, bq, Wk, bk, Wv, bv, gamma, beta):
        import jax, jax.numpy as jnp
        import numpy as np
        HIDDEN = 256
        NHEADS = 8
        ALPHA = 0.1
        NUM_HOP = 4
        MASK_VAL = -16384.0
        LN_EPS = 1e-05
        B, N, H = x.shape
        u = H // NHEADS
        q = x @ Wq.T + bq
        k = x @ Wk.T + bk
        v = x @ Wv.T + bv
        qh = q.reshape(B, N, NHEADS, u).transpose(0, 2, 1, 3)
        kh = k.reshape(B, N, NHEADS, u).transpose(0, 2, 1, 3)
        vh = v.reshape(B, N, NHEADS, u).transpose(0, 2, 1, 3)
        scores = jnp.einsum('bhnd,bhmd->bhnm', qh, kh)
        mask = (adj == 0)[:, None, :, :]
        scores = jnp.where(mask, MASK_VAL, scores)
        pros = jax.nn.softmax(scores, axis=-1)
        z_init = vh
        z = z_init
        for _ in range(NUM_HOP):
            z = (1.0 - ALPHA) * jnp.einsum('bhnm,bhmd->bhnd', pros, z) + ALPHA * z_init
        h_prime = z.transpose(0, 2, 1, 3).reshape(B, N, H)
        y = x + h_prime
        mu = jnp.mean(y, axis=-1, keepdims=True)
        var = jnp.mean((y - mu) ** 2, axis=-1, keepdims=True)
        return (y - mu) / jnp.sqrt(var + LN_EPS) * gamma + beta
    x = _L0_gnn_ref(x, adj, L0_gnn_Wq, L0_gnn_bq, L0_gnn_Wk, L0_gnn_bk, L0_gnn_Wv, L0_gnn_bv, L0_gnn_Wo, L0_gnn_bo, L0_gnn_gamma, L0_gnn_beta)
    x = _L1_gnn_ref(x, adj, L1_gnn_Wq, L1_gnn_bq, L1_gnn_Wk, L1_gnn_bk, L1_gnn_Wv, L1_gnn_bv, L1_gnn_gamma, L1_gnn_beta)
    return x

_drawn_inputs = setup_inputs


def setup_inputs(seed=0):
    import zlib

    import numpy as np

    out = dict(_drawn_inputs(seed))
    spreads = {'L0_gnn_bq': (0.0, 0.8),
     'L0_gnn_bk': (0.0, 0.8),
     'L0_gnn_bv': (0.0, 0.1),
     'L0_gnn_bo': (0.0, 0.1),
     'L0_gnn_gamma': (1.0, 0.2),
     'L0_gnn_beta': (0.0, 0.1),
     'L1_gnn_gamma': (1.0, 0.2),
     'L1_gnn_beta': (0.0, 0.1)}
    factors = {'L1_gnn_bq': 6.282, 'L1_gnn_bk': 8.0}
    for name, (base, spread) in spreads.items():
        noise = np.random.default_rng([zlib.crc32(name.encode()), seed]).standard_normal(out[name].shape)
        drawn = base * np.exp(spread * noise) if base else spread * noise
        out[name] = jnp.asarray(drawn.astype(out[name].dtype))
    for name, factor in factors.items():
        out[name] = (out[name] * factor).astype(out[name].dtype)
    return out
```

```python
from contextlib import ExitStack

import numpy as np
import concourse.bass as bass
from concourse import mybir

FP32 = mybir.dt.float32
F32R = mybir.dt.float32r
I32 = mybir.dt.int32
ALU = mybir.AluOpType
ACT = mybir.ActivationFunctionType

B, N, D, H = 64, 128, 256, 8
HD = D // H
G = 4
C = D // 128
T = 2 * N
PAIRS = B // 2
NUM_HOP = 4
ALPHA = 0.1
LN_EPS = 1e-05
SCALE = 1.0 / float(np.sqrt(HD))
MASKED = -1.0e30
BIG = 3.0e38
SPARE = 2


class Pair:

    def __init__(self, i, c):
        self.i, self.c = i, c

    def __add__(self, d):
        return Pair(self.i, self.c + d)

    def __sub__(self, d):
        return Pair(self.i, self.c - d)

    @property
    def parity(self):
        return self.c % 2

    @property
    def half(self):
        return self.i + self.c // 2

    @property
    def number(self):
        return self.i * 2 + self.c


class Count:

    def __init__(self, sem, per):
        self.sem, self.per = sem, per

    def at(self, pair, j=None):
        j = self.per if j is None else j
        return pair.i * (2 * self.per) + self.per * (pair.c + SPARE) + j


class DmaCount:

    def __init__(self, sems, dmas):
        self.sems, self.per = sems, 16 * dmas

    def sem(self, pair):
        return self.sems[pair.parity]

    def at(self, pair):
        return pair.half * self.per + 2 * self.per


def two_layers(nc, x, x_t, adj, w, rows, cols, ident_d, out):
    ctx = ExitStack()
    with ctx:
        def sb(name, shape, dt=FP32):
            return ctx.enter_context(nc.sbuf_tensor(name, shape, dt))

        def bank(name, n=1):
            return ctx.enter_context(nc.psum_tensor(name, [128, 512 * n], FP32))

        owned = {}

        def count(name, per=1, by=None):
            c = Count(ctx.enter_context(nc.semaphore(name)), per)
            owned.setdefault(by, []).append(c)
            return c

        def sem(name):
            return ctx.enter_context(nc.semaphore(name))

        NW = 7
        w_raw = sb("w_raw", [128, NW, C, D])
        w_hi = sb("w_hi", [128, NW, C, D], F32R)
        w_lo = sb("w_lo", [128, NW, C, D], F32R)
        row = sb("row", [128, 7, D])
        col = sb("col", [128, 4, C])
        bq0s = sb("bq0s", [128, C])
        ident = sb("ident", [128, 128])
        mhalf = sb("mhalf", [128, 2])
        BV0, BO0, GA0, BE0, BV1, GA1, BE1 = range(7)

        xt_in = [sb(f"xt_in{i}", [128, C, T]) for i in range(2)]
        x_in = [sb(f"x_in{i}", [128, 2, D]) for i in range(2)]
        adj_in = [sb(f"adj_in{i}", [128, 2, N], I32) for i in range(2)]
        mask = [sb(f"mask{i}", [128, 2, N]) for i in range(2)]

        xh = [sb(f"xh{l}", [128, C, T], F32R) for l in range(2)]
        xl = [sb(f"xl{l}", [128, C, T], F32R) for l in range(2)]
        qT = [sb(f"qT{l}", [128, C, T]) for l in range(2)]
        kT = [sb(f"kT{l}", [128, C, T]) for l in range(2)]
        v = [sb(f"v{l}", [128, 2, D]) for l in range(2)]
        sm = [sb(f"sm{l}", [128, 2, H, N]) for l in range(2)]
        nmax = [sb(f"nmax{l}", [128, 2, H]) for l in range(2)]
        ex = [sb(f"ex{l}", [128, 2, H, N]) for l in range(2)]
        tot = [sb(f"tot{l}", [128, 2, H]) for l in range(2)]
        rec = [sb(f"rec{l}", [128, 2, H]) for l in range(2)]
        pr = [sb(f"pr{l}", [128, 2, H, N]) for l in range(2)]
        pT = [sb(f"pT{l}", [128, 2, H, N]) for l in range(2)]
        bst = [sb(f"bst{l}", [128, 2, 6]) for l in range(2)]
        mv = [sb(f"mv{l}", [128, 2, 2]) for l in range(2)]
        ve = [sb(f"ve{l}", [128, 2]) for l in range(2)]
        rstd = [sb(f"rstd{l}", [128, 2]) for l in range(2)]
        y = [sb(f"y{l}", [128, 2, D]) for l in range(2)]
        yn = [sb(f"yn{l}", [128, 2, D]) for l in range(2)]
        yg = [sb(f"yg{l}", [128, 2, D]) for l in range(2)]
        oh = sb("oh", [128, 2 * C, N], F32R)
        ol = sb("ol", [128, 2 * C, N], F32R)
        xb = sb("xb", [128, 2, D])
        x1 = [sb(f"x1_{i}", [128, 2, D]) for i in range(2)]
        z0s = sb("z0s", [128, 2, D])
        zf = sb("zf", [128, 2, D])
        hT = [sb(f"hT{b}", [128, C, N]) for b in range(2)]
        z = [sb(f"z{b}", [128, D]) for b in range(2)]
        o_t = [sb(f"o_t{i}", [128, 2, D]) for i in range(2)]

        psS = bank("psS", 4)
        psT = [bank(f"psT{i}") for i in range(2)]
        psM = [bank(f"psM{i}") for i in range(2)]

        qr = [count(f"q{l}_ready", 1, "pe") for l in range(2)]
        kr = [count(f"k{l}_ready", 1, "pe") for l in range(2)]
        vr = [count(f"v{l}_ready", 1, "pe") for l in range(2)]
        sr = [count(f"s{l}_ready", 1, "pe") for l in range(2)]
        tr = [count(f"pT{l}_ready", 4, "pe") for l in range(2)]
        avr = count("av_ready", 1, "pe")
        wor = count("wo_ready", 1, "pe")
        x1r = count("x1T_ready", 1, "pe")
        hr = count("hopT_ready", 2 * NUM_HOP, "pe")
        zr = count("hop_ready", 2 * NUM_HOP, "pe")

        q_s = [count(f"q{l}_saved", 1, "act") for l in range(2)]
        exps = [count(f"exp{l}_done", 2, "act") for l in range(2)]
        pT_s = [count(f"pT{l}_saved", 4, "act") for l in range(2)]
        oh_s = count("oh_saved", 1, "act")
        x1h_s = count("x1h_saved", 1, "act")
        hT_s = count("hopT_saved", 2 * NUM_HOP, "act")

        k_s = [count(f"k{l}_saved", 1, "dve") for l in range(2)]
        v_s = [count(f"v{l}_saved", 1, "dve") for l in range(2)]
        mx = [count(f"masked{l}_done", 4, "dve") for l in range(2)]
        rec_s = [count(f"rec{l}_done", 2, "dve") for l in range(2)]
        tmp_s = count("rec1_raw_done", 2, "dve")
        xh_s = count("xh_saved", 1, "dve")
        xl_s = count("xl_saved", 1, "dve")
        mask_s = count("mask_done", 1, "dve")
        ol_s = count("ol_saved", 1, "dve")
        y_s = count("y0_saved", 1, "dve")
        bn_s = [count(f"bn{l}_done", 1, "dve") for l in range(2)]
        ag_s = [count(f"aggr{l}_done", 1, "dve") for l in range(2)]
        ve_s = [count(f"var_eps{l}_done", 1, "dve") for l in range(2)]
        yn_s = [count(f"normed{l}_done", 1, "dve") for l in range(2)]
        yg_s = count("gamma0_done", 1, "dve")
        x1_s = count("x1_done", 1, "dve")
        x1l_s = count("x1l_saved", 1, "dve")
        z_s = count("hop_saved", 2 * NUM_HOP, "dve")

        xb_s = count("xb_done", 1, "pool")
        pr_s = [count(f"probs{l}_done", 2, "pool") for l in range(2)]
        rstd_s = [count(f"rstd{l}_done", 1, "pool") for l in range(2)]
        z0_s = count("z0s_done", 1, "pool")
        zf_s = count("zf_done", 1, "pool")
        g1_s = count("gamma1_done", 1, "pool")
        o_s = count("out_done", 1, "pool")

        in_s = DmaCount([sem("in_even"), sem("in_odd")], 3)
        st_s = DmaCount([sem("store_even"), sem("store_odd")], 1)
        w_in = [sem(f"w_in{i}") for i in range(NW)]
        c_in = sem("const_in")
        wh_s = sem("w_hi_done")
        wl_s = sem("w_lo_done")
        bq_s = sem("bq0s_done")
        mh_s = sem("mhalf_done")
        own = sem("own_instruction")

        block = ctx.enter_context(nc.Block())

        def credit(eng, who):
            for c in owned[who]:
                eng.sem_inc(c.sem, c.per * SPARE)

        def pipeline(eng, step, peel=0):
            step(Pair(0, -1), False, False, True)
            step(Pair(0, 0), False, True, True)
            turns = (PAIRS - 2) // 2 - peel
            with eng.Fori(0, turns) as i:
                for u in range(2):
                    step(Pair(i, 1 + u), True, True, True)
            for t in range(1 + 2 * turns, PAIRS - 1):
                step(Pair(0, t), True, True, True)
            step(Pair(0, PAIRS - 1), True, True, False)
            step(Pair(0, PAIRS), True, False, False)

        def both(row_i):
            return row[:, row_i:row_i + 1, :].broadcast_to([128, 2, D])

        @block.sync
        def _(sp):
            for s in st_s.sems:
                sp.sem_inc(s, 16)
            for s in in_s.sems:
                sp.sem_inc(s, in_s.per)

            def load(p):
                sp.wait_ge(xl_s.sem, xl_s.at(p - 2))
                sp.wait_ge(xb_s.sem, xb_s.at(p - 2))
                sp.wait_ge(mask_s.sem, mask_s.at(p - 2))
                i = p.parity
                sp.dma_start(xt_in[i][:, :, :], x_t[bass.ds(p.number, 1)].rearrange("a p c t -> (a p) c t")
                             ).then_inc(in_s.sem(p), 16)
                sp.dma_start(adj_in[i][:, :, :], adj[bass.ds(p.number * 2, 2)].rearrange("b n m -> n b m")
                             ).then_inc(in_s.sem(p), 16)
                sp.dma_start(x_in[i][:, :, :], x[bass.ds(p.number * 2, 2)].rearrange("b n d -> n b d")
                             ).then_inc(in_s.sem(p), 16)

            load(Pair(0, 0))
            for i in range(NW):
                if i == 3:
                    sp.dma_start(col[:, :, :], cols).then_inc(c_in, 16)
                    sp.dma_start(row[:, :, :], rows.partition_broadcast(128)).then_inc(c_in, 16)
                    sp.dma_start(ident[:, :], ident_d).then_inc(c_in, 16)
                sp.dma_start(w_raw[:, i, :, :], w[i].rearrange("(c p) o -> p c o", p=128)).then_inc(w_in[i], 16)
            load(Pair(0, 1))

            def step(t, layer1, finish0, start0):
                if start0 and not (isinstance(t.i, int) and (t.c < 0 or t.c + 2 >= PAIRS)):
                    load(t + 2)
                if layer1:
                    p = t - 1
                    sp.wait_ge(o_s.sem, o_s.at(p))
                    sp.dma_start(out[bass.ds(p.number * 2, 2)].rearrange("b n d -> n b d"), o_t[p.parity][:, :, :]
                                 ).then_inc(st_s.sem(p), 16)

            pipeline(sp, step, peel=1)
            for p in (Pair(0, PAIRS - 2), Pair(0, PAIRS - 1)):
                sp.wait_ge(st_s.sem(p), st_s.at(p))

        @block.tensor
        def _(pe):
            credit(pe, "pe")
            parts = ((0, 0), (1, 0), (0, 1))

            def project_T(l, wi, dst):
                x_p, w_p = (xh[l], xl[l]), (w_hi, w_lo)
                for c in range(C):
                    for n, (a, e) in enumerate(parts):
                        for kc in range(C):
                            last = nc.tensor.matmul(dst[:, c * T:(c + 1) * T],
                                                    w_p[e][:, wi, kc, c * 128:(c + 1) * 128],
                                                    x_p[a][:, kc, :], start=(n == 0 and kc == 0),
                                                    stop=(n == 2 and kc == C - 1))
                return last

            def project(l, wi, dst):
                x_p, w_p = (xh[l], xl[l]), (w_hi, w_lo)
                for b in range(2):
                    for n, (a, e) in enumerate(parts):
                        for kc in range(C):
                            last = nc.tensor.matmul(dst[:, b * D:(b + 1) * D],
                                                    x_p[a][:, kc, b * N:(b + 1) * N],
                                                    w_p[e][:, wi, kc, :], start=(n == 0 and kc == 0),
                                                    stop=(n == 2 and kc == C - 1))
                return last

            def scores(l):
                for b in range(2):
                    for c in range(C):
                        for g in range(G):
                            r = slice(32 * g, 32 * g + 32)
                            o = 512 * g + (b * C + c) * N
                            last = nc.tensor.matmul(psS[:, o:o + N], qT[l][r, c, b * N:(b + 1) * N],
                                                    kT[l][r, c, b * N:(b + 1) * N], start=True, stop=True)
                return last

            def turn_probs(l, p, b, c):
                for g in range(G):
                    last = nc.tensor.transpose(psT[c][:, g * N:(g + 1) * N], pr[l][:, b, G * c + g, :], ident[:, :])
                last.then_inc(tr[l].sem, 1)

            def spread(l, b, src, dst, off):
                for c in range(C):
                    for g in range(G):
                        h = G * c + g
                        last = nc.tensor.matmul(dst[32 * g:32 * g + 32, off + c * N:off + (c + 1) * N],
                                                src[:, h * HD:(h + 1) * HD], pT[l][:, b, h, :],
                                                start=True, stop=True)
                return last

            def step(t, layer1, finish0, start0):
                p, n = t - 1, t + 1
                if layer1:
                    pe.wait_ge(x1l_s.sem, x1l_s.at(p))
                    pe.wait_ge(hT_s.sem, hT_s.at(p - 1))
                    if isinstance(p.i, int) and p.c == 0 or not isinstance(p.i, int):
                        pe.wait_ge(wh_s, NW)
                        pe.wait_ge(wl_s, NW)
                    project_T(1, 4, psM[0]).then_inc(qr[1].sem, 1)
                    if start0 or finish0:
                        pe.wait_ge(v_s[0].sem, v_s[0].at(t))
                    project_T(1, 5, psM[1]).then_inc(kr[1].sem, 1)
                    pe.wait_ge(q_s[1].sem, q_s[1].at(p))
                    project(1, 6, psM[0]).then_inc(vr[1].sem, 1)
                    pe.wait_ge(k_s[1].sem, k_s[1].at(p))
                    if finish0:
                        pe.wait_ge(mx[0].sem, mx[0].at(t))
                    scores(1).then_inc(sr[1].sem, 1)
                if finish0:
                    pe.wait_ge(z_s.sem, z_s.at(p - 1))
                    for b in range(2):
                        pe.wait_ge(pr_s[0].sem, pr_s[0].at(t, b + 1))
                        for c in range(C):
                            if b:
                                pe.wait_ge(pT_s[0].sem, pT_s[0].at(t, c + 1))
                            turn_probs(0, t, b, c)
                    pe.wait_ge(v_s[0].sem, v_s[0].at(t))
                    if layer1:
                        pe.wait_ge(k_s[1].sem, k_s[1].at(p))
                    pe.wait_ge(pT_s[0].sem, pT_s[0].at(t))
                    for b in range(2):
                        last = spread(0, b, v[0][:, b, :], psM[1], b * C * N)
                    last.then_inc(avr.sem, 1)
                if layer1:
                    pe.wait_ge(v_s[1].sem, v_s[1].at(p))
                if start0:
                    if isinstance(t.i, int) and t.c < 0:
                        pe.wait_ge(wh_s, 3)
                        pe.wait_ge(wl_s, 3)
                    pe.wait_ge(xl_s.sem, xl_s.at(n))
                    if finish0 and not layer1:
                        pe.wait_ge(x1l_s.sem, x1l_s.at(t - 1))
                    project_T(0, 0, psM[0]).then_inc(qr[0].sem, 1)
                    pe.wait_ge(ol_s.sem, ol_s.at(t))
                    project_T(0, 1, psM[1]).then_inc(kr[0].sem, 1)
                    pe.wait_ge(q_s[0].sem, q_s[0].at(n))
                if finish0:
                    if isinstance(t.i, int) and t.c == 0:
                        pe.wait_ge(wh_s, 4)
                        pe.wait_ge(wl_s, 4)
                    pe.wait_ge(ol_s.sem, ol_s.at(t))
                    o_p, w_p = (oh, ol), (w_hi, w_lo)
                    for b in range(2):
                        for m, (a, e) in enumerate(parts):
                            for c in range(C):
                                last = nc.tensor.matmul(psM[0][:, b * D:(b + 1) * D], o_p[a][:, b * C + c, :],
                                                        w_p[e][:, 3, c, :], start=(m == 0 and c == 0),
                                                        stop=(m == 2 and c == C - 1))
                    last.then_inc(wor.sem, 1)
                if start0:
                    pe.wait_ge(k_s[0].sem, k_s[0].at(n))
                    project(0, 2, psM[1]).then_inc(vr[0].sem, 1)
                    pe.wait_ge(mx[1].sem, mx[1].at(p))
                    scores(0).then_inc(sr[0].sem, 1)
                if layer1:
                    for b in range(2):
                        pe.wait_ge(pr_s[1].sem, pr_s[1].at(p, b + 1))
                        for c in range(C):
                            if b:
                                pe.wait_ge(pT_s[1].sem, pT_s[1].at(p, c + 1))
                            turn_probs(1, p, b, c)
                if finish0:
                    pe.wait_ge(x1_s.sem, x1_s.at(t))
                    for kc in range(C):
                        for b in range(2):
                            o = kc * T + b * N
                            last = nc.tensor.transpose(psM[0][:, o:o + N], x1[t.parity][:, b, kc * 128:(kc + 1) * 128],
                                                       ident[:, :])
                    last.then_inc(x1r.sem, 1)
                if layer1:
                    pe.wait_ge(pT_s[1].sem, pT_s[1].at(p))
                    for j in range(NUM_HOP):
                        for b in range(2):
                            if j:
                                pe.wait_ge(z_s.sem, z_s.at(p, 2 * j - 1 + b))
                            elif b == 0:
                                if finish0:
                                    pe.wait_ge(x1l_s.sem, x1l_s.at(t))
                            elif start0:
                                pe.wait_ge(v_s[0].sem, v_s[0].at(n))
                            src = z[b][:, :] if j else v[1][:, b, :]
                            spread(1, b, src, psM[b], 0).then_inc(hr.sem, 1)
                        for b in range(2):
                            pe.wait_ge(hT_s.sem, hT_s.at(p, 2 * j + 1 + b))
                            for c in range(C):
                                last = nc.tensor.transpose(psT[b][:, c * 128:(c + 1) * 128], hT[b][:, c, :], ident[:, :])
                            last.then_inc(zr.sem, 1)

            pe.wait_ge(c_in, 48)
            pipeline(pe, step)

        @block.scalar
        def _(act):
            credit(act, "act")
            for i in range(NW):
                act.wait_ge(w_in[i], 16)
                nc.scalar.activation(w_hi[:, i, :, :], w_raw[:, i, :, :], ACT.Copy).then_inc(wh_s, 1)
            act.wait_ge(c_in, 48)
            act.wait_ge(bq_s, 1)

            def save_q(l, p, ps):
                act.wait_ge(qr[l].sem, qr[l].at(p))
                act.wait_ge(sr[l].sem, sr[l].at(p - 1))
                for c in range(C):
                    b = bq0s[:, c:c + 1] if l == 0 else col[:, 2, c:c + 1]
                    last = nc.scalar.activation(qT[l][:, c, :], ps[:, c * T:(c + 1) * T], ACT.Identity, bias=b,
                                                scale=SCALE if l == 0 else 1.0)
                last.then_inc(q_s[l].sem, 1)

            def exp_head(l, p, b, h):
                if h == 0:
                    act.wait_ge(pr_s[l].sem, pr_s[l].at(p - 1, b + 1))
                if h % 4 == 0:
                    act.wait_ge(mx[l].sem, mx[l].at(p, 2 * b + h // 4 + 1))
                e = nc.scalar.activation(ex[l][:, b, h, :], sm[l][:, b, h, :], ACT.Exp, scale=-1.0,
                                         bias=nmax[l][:, b, h:h + 1], accum_out=tot[l][:, b, h:h + 1])
                if h == H - 1:
                    e.then_inc(exps[l].sem, 1)

            def save_pT(l, p, b, c):
                act.wait_ge(tr[l].sem, tr[l].at(p, 2 * b + c + 1))
                nc.scalar.activation(pT[l][:, b, G * c:G * c + G, :],
                                     psT[c][:, :].rearrange("p (g n) -> p g n", g=G), ACT.Copy
                                     ).then_inc(pT_s[l].sem, 1)

            def step(t, layer1, finish0, start0):
                p, n = t - 1, t + 1
                if finish0:
                    for h in range(3):
                        exp_head(0, t, 1, h)
                if layer1:
                    save_q(1, p, psM[0])
                if finish0:
                    for h in range(3, H):
                        exp_head(0, t, 1, h)
                    act.wait_ge(avr.sem, avr.at(t - 1))
                    for b in range(2):
                        for c in range(C):
                            save_pT(0, t, b, c)
                    act.wait_ge(avr.sem, avr.at(t))
                    act.wait_ge(wor.sem, wor.at(t - 1))
                    nc.scalar.activation(oh[:, :, :], psM[1][:, :].rearrange("p (a n) -> p a n", n=N), ACT.Copy
                                         ).then_inc(oh_s.sem, 1)
                if start0:
                    save_q(0, n, psM[0])
                if layer1:
                    for b in range(2):
                        for h in range(H):
                            exp_head(1, p, b, h)
                    act.wait_ge(hr.sem, hr.at(p - 1))
                    for b in range(2):
                        for c in range(C):
                            save_pT(1, p, b, c)
                if finish0:
                    act.wait_ge(x1r.sem, x1r.at(t))
                    act.wait_ge(vr[1].sem, vr[1].at(t - 1))
                    nc.scalar.activation(xh[1][:, :, :], psM[0][:, :].rearrange("p (c t) -> p c t", c=C), ACT.Copy
                                         ).then_inc(x1h_s.sem, 1)
                for j in range(NUM_HOP):
                    for b in range(2):
                        if layer1:
                            act.wait_ge(hr.sem, hr.at(p, 2 * j + b + 1))
                            if j == 0:
                                act.wait_ge(zr.sem, zr.at(p - 1))
                            else:
                                act.wait_ge(zr.sem, zr.at(p, 2 * j - 1 + b))
                            nc.scalar.activation(hT[b][:, :, :], psM[b][:, 0:C * N].rearrange("p (c n) -> p c n", c=C),
                                                 ACT.Copy).then_inc(hT_s.sem, 1)
                        if start0:
                            exp_head(0, n, 0, 2 * j + b)

            pipeline(act, step)

        @block.vector
        def _(dve):
            credit(dve, "dve")
            dve.wait_ge(c_in, 48)
            nc.vector.tensor_scalar(bq0s[:, :], col[:, 0, :], SCALE, None, ALU.mult).then_inc(bq_s, 1)

            def split_w(i):
                dve.wait_ge(wh_s, i + 1)
                nc.vector.tensor_tensor(w_lo[:, i, :, :], w_raw[:, i, :, :], w_hi[:, i, :, :].bitcast(FP32), ALU.subtract
                                        ).then_inc(wl_s, 1)

            def split_x(p):
                dve.wait_ge(in_s.sem(p), in_s.at(p))
                dve.wait_ge(vr[0].sem, vr[0].at(p - 1))
                nc.vector.tensor_copy(xh[0][:, :, :], xt_in[p.parity][:, :, :]).then_inc(xh_s.sem, 1)
                dve.wait_ge(xh_s.sem, xh_s.at(p))
                nc.vector.tensor_tensor(xl[0][:, :, :], xt_in[p.parity][:, :, :], xh[0][:, :, :].bitcast(FP32),
                                        ALU.subtract).then_inc(xl_s.sem, 1)

            def make_mask(p):
                dve.wait_ge(mx[1].sem, mx[1].at(p - 2))
                nc.vector.tensor_scalar(mask[p.parity][:, :, :], adj_in[p.parity][:, :, :], 0.0, MASKED,
                                        ALU.is_equal, ALU.mult).then_inc(mask_s.sem, 1)

            def save_k(l, p, ps):
                dve.wait_ge(kr[l].sem, kr[l].at(p))
                dve.wait_ge(sr[l].sem, sr[l].at(p - 1))
                for c in range(C):
                    last = nc.vector.tensor_scalar(kT[l][:, c, :], ps[:, c * T:(c + 1) * T],
                                                   col[:, 2 * l + 1, c:c + 1], None, ALU.add)
                last.then_inc(k_s[l].sem, 1)

            def save_v(l, p, ps):
                dve.wait_ge(vr[l].sem, vr[l].at(p))
                if l == 0:
                    dve.wait_ge(avr.sem, avr.at(p - 1))
                else:
                    dve.wait_ge(hr.sem, hr.at(p - 1))
                    dve.wait_ge(z0_s.sem, z0_s.at(p - 1))
                nc.vector.tensor_tensor(v[l][:, :, :], ps[:, :].rearrange("p (b d) -> p b d", b=2),
                                        both(BV1 if l else BV0), ALU.add).then_inc(v_s[l].sem, 1)

            def mask_scores(l, p):
                dve.wait_ge(sr[l].sem, sr[l].at(p))
                dve.wait_ge(mask_s.sem, mask_s.at(p))
                dve.wait_ge(exps[l].sem, exps[l].at(p - 1))
                dve.sem_inc(own, 1)
                for b in range(2):
                    for c in range(C):
                        for g in range(G):
                            h, o = G * c + g, 512 * g + (b * C + c) * N
                            last = nc.vector.tensor_tensor_reduce(
                                sm[l][:, b, h, :], psS[:, o:o + N], mask[p.parity][:, b, :], -1.0, BIG,
                                ALU.add, ALU.min, nmax[l][:, b, h:h + 1])
                        last.then_inc(mx[l].sem, 1)

            def reciprocals(l, p, b):
                dve.wait_ge(exps[l].sem, exps[l].at(p, b + 1))
                dve.wait_ge(pr_s[l].sem, pr_s[l].at(p - 1, b + 1))
                r = nc.vector.reciprocal(rec[l][:, b, :], tot[l][:, b, :])
                if l:
                    r.then_inc(tmp_s.sem, 1)
                    dve.wait_ge(tmp_s.sem, tmp_s.at(p, b + 1))
                    r = nc.vector.tensor_scalar(rec[l][:, b, :], rec[l][:, b, :], 1.0 - ALPHA, None, ALU.mult)
                r.then_inc(rec_s[l].sem, 1)

            def statistics(l, p):
                for b in range(2):
                    last = nc.vector.bn_stats(bst[l][:, b, :], y[l][:, b, :])
                last.then_inc(bn_s[l].sem, 1)
                dve.wait_ge(bn_s[l].sem, bn_s[l].at(p))
                dve.sem_inc(own, 1)
                for b in range(2):
                    last = nc.vector.bn_aggr(mv[l][:, b, :], bst[l][:, b, :])
                last.then_inc(ag_s[l].sem, 1)
                dve.wait_ge(ag_s[l].sem, ag_s[l].at(p))
                dve.wait_ge(rstd_s[l].sem, rstd_s[l].at(p - 1))
                nc.vector.tensor_scalar(ve[l][:, :], mv[l][:, :, 1], LN_EPS, None, ALU.add).then_inc(ve_s[l].sem, 1)

            def normalise(l, p):
                dve.wait_ge(rstd_s[l].sem, rstd_s[l].at(p))
                if l:
                    dve.wait_ge(g1_s.sem, g1_s.at(p - 1))
                for b in range(2):
                    last = nc.vector.tensor_scalar(yn[l][:, b, :], y[l][:, b, :], mv[l][:, b, 0:1], rstd[l][:, b:b + 1],
                                                   ALU.subtract, ALU.mult)
                last.then_inc(yn_s[l].sem, 1)

            def step(t, layer1, finish0, start0):
                p, n = t - 1, t + 1
                if layer1:
                    save_k(1, p, psM[1])
                    save_v(1, p, psM[0])
                if finish0:
                    reciprocals(0, t, 1)
                if start0:
                    split_x(n)
                if layer1:
                    mask_scores(1, p)
                if start0:
                    make_mask(n)
                if finish0:
                    dve.wait_ge(oh_s.sem, oh_s.at(t))
                    dve.wait_ge(wor.sem, wor.at(t - 1))
                    nc.vector.tensor_tensor(ol[:, :, :], psM[1][:, :].rearrange("p (a n) -> p a n", n=N),
                                            oh[:, :, :].bitcast(FP32), ALU.subtract).then_inc(ol_s.sem, 1)
                if start0:
                    save_k(0, n, psM[1])
                if finish0:
                    dve.wait_ge(wor.sem, wor.at(t))
                    dve.wait_ge(xb_s.sem, xb_s.at(t))
                    nc.vector.tensor_tensor(y[0][:, :, :], psM[0][:, :].rearrange("p (b d) -> p b d", b=2), xb[:, :, :],
                                            ALU.add).then_inc(y_s.sem, 1)
                    dve.wait_ge(y_s.sem, y_s.at(t))
                    statistics(0, t)
                if start0:
                    save_v(0, n, psM[1])
                if finish0:
                    normalise(0, t)
                    dve.wait_ge(yn_s[0].sem, yn_s[0].at(t))
                    nc.vector.tensor_tensor(yg[0][:, :, :], yn[0][:, :, :], both(GA0), ALU.mult).then_inc(yg_s.sem, 1)
                    dve.wait_ge(yg_s.sem, yg_s.at(t))
                    dve.wait_ge(x1r.sem, x1r.at(t - 2))
                    dve.wait_ge(zf_s.sem, zf_s.at(t - 2))
                    nc.vector.tensor_tensor(x1[t.parity][:, :, :], yg[0][:, :, :], both(BE0), ALU.add
                                            ).then_inc(x1_s.sem, 1)
                if layer1:
                    reciprocals(1, p, 0)
                    reciprocals(1, p, 1)
                if start0:
                    mask_scores(0, n)
                if finish0:
                    dve.wait_ge(x1h_s.sem, x1h_s.at(t))
                    nc.vector.tensor_tensor(xl[1][:, :, :], psM[0][:, :].rearrange("p (c t) -> p c t", c=C),
                                            xh[1][:, :, :].bitcast(FP32), ALU.subtract).then_inc(x1l_s.sem, 1)
                if layer1:
                    dve.wait_ge(zf_s.sem, zf_s.at(p))
                    for j in range(NUM_HOP):
                        for b in range(2):
                            dve.wait_ge(zr.sem, zr.at(p, 2 * j + b + 1))
                            end = j == NUM_HOP - 1
                            nc.vector.tensor_tensor(y[1][:, b, :] if end else z[b][:, :], psT[b][:, 0:D],
                                                    zf[:, b, :] if end else z0s[:, b, :], ALU.add
                                                    ).then_inc(z_s.sem, 1)
                    dve.wait_ge(z_s.sem, z_s.at(p))
                    statistics(1, p)
                if start0:
                    reciprocals(0, n, 0)
                if layer1:
                    normalise(1, p)

            for i in range(4):
                split_w(i)
            split_x(Pair(0, 0))
            make_mask(Pair(0, 0))
            for i in range(4, NW):
                split_w(i)

            def first_or_step(t, layer1, finish0, start0):
                if isinstance(t.i, int) and t.c < 0:
                    save_k(0, t + 1, psM[1])
                    save_v(0, t + 1, psM[1])
                    mask_scores(0, t + 1)
                    reciprocals(0, t + 1, 0)
                else:
                    step(t, layer1, finish0, start0)

            pipeline(dve, first_or_step)

        @block.gpsimd
        def _(pool):
            credit(pool, "pool")
            nc.gpsimd.memset(mhalf[:, :], -0.5).then_inc(mh_s, 1)
            pool.wait_ge(mh_s, 1)
            pool.wait_ge(c_in, 48)

            def probabilities(l, p, b):
                pool.wait_ge(rec_s[l].sem, rec_s[l].at(p, b + 1))
                pool.wait_ge(tr[l].sem, tr[l].at(p - 1, 2 * b + 2))
                nc.gpsimd.tensor_tensor(pr[l][:, b, :, :], ex[l][:, b, :, :],
                                        rec[l][:, b, :].unsqueeze(2).broadcast_to([128, H, N]), ALU.mult
                                        ).then_inc(pr_s[l].sem, 1)

            def inverse_root(l, p):
                pool.wait_ge(ve_s[l].sem, ve_s[l].at(p))
                pool.wait_ge(yn_s[l].sem, yn_s[l].at(p - 1))
                nc.gpsimd.tensor_tensor(rstd[l][:, :], ve[l][:, :], mhalf[:, :], ALU.pow).then_inc(rstd_s[l].sem, 1)

            def step(t, layer1, finish0, start0):
                p, n = t - 1, t + 1
                if finish0:
                    pool.wait_ge(in_s.sem(t), in_s.at(t))
                    pool.wait_ge(y_s.sem, y_s.at(t - 1))
                    nc.gpsimd.tensor_tensor(xb[:, :, :], x_in[t.parity][:, :, :], both(BO0), ALU.add
                                            ).then_inc(xb_s.sem, 1)
                    probabilities(0, t, 1)
                if layer1:
                    pool.wait_ge(v_s[1].sem, v_s[1].at(p))
                    pool.wait_ge(z_s.sem, z_s.at(p - 1))
                    pool.sem_inc(own, 1)
                    nc.gpsimd.tensor_scalar(z0s[:, :, :], v[1][:, :, :], ALPHA, 0.0, ALU.mult, ALU.add
                                            ).then_inc(z0_s.sem, 1)
                    pool.wait_ge(z0_s.sem, z0_s.at(p))
                    pool.wait_ge(x1_s.sem, x1_s.at(p))
                    nc.gpsimd.tensor_tensor(zf[:, :, :], z0s[:, :, :], x1[p.parity][:, :, :], ALU.add
                                            ).then_inc(zf_s.sem, 1)
                if finish0:
                    inverse_root(0, t)
                if layer1:
                    probabilities(1, p, 0)
                    probabilities(1, p, 1)
                    inverse_root(1, p)
                if start0:
                    probabilities(0, n, 0)
                if layer1:
                    pool.wait_ge(yn_s[1].sem, yn_s[1].at(p))
                    nc.gpsimd.tensor_tensor(yg[1][:, :, :], yn[1][:, :, :], both(GA1), ALU.mult).then_inc(g1_s.sem, 1)
                    pool.wait_ge(g1_s.sem, g1_s.at(p))
                    pool.wait_ge(st_s.sem(p), st_s.at(p - 2))
                    nc.gpsimd.tensor_tensor(o_t[p.parity][:, :, :], yg[1][:, :, :], both(BE1), ALU.add
                                            ).then_inc(o_s.sem, 1)

            pipeline(pool, step)


def kernel(**inputs):
    from concourse import bacc
    from concourse.bass_utils import run_bass_kernel_spmd

    def arr(name):
        return np.ascontiguousarray(inputs[name])

    x = arr("x")
    x_t = np.ascontiguousarray(x.reshape(PAIRS, T, C, 128).transpose(0, 3, 2, 1))
    w = np.stack([arr("L0_gnn_Wq"), arr("L0_gnn_Wk"), arr("L0_gnn_Wv"), arr("L0_gnn_Wo"),
                  arr("L1_gnn_Wq").T, arr("L1_gnn_Wk").T, arr("L1_gnn_Wv").T])
    rows = np.stack([arr(n) for n in ("L0_gnn_bv", "L0_gnn_bo", "L0_gnn_gamma", "L0_gnn_beta",
                                      "L1_gnn_bv", "L1_gnn_gamma", "L1_gnn_beta")])
    cols = np.ascontiguousarray(np.stack([arr(n).reshape(C, 128) for n in (
        "L0_gnn_bq", "L0_gnn_bk", "L1_gnn_bq", "L1_gnn_bk")]).transpose(2, 0, 1))
    ident = np.eye(128, dtype=np.float32)
    arrays = {"in_x": x, "in_x_t": x_t, "in_adj": arr("adj"), "in_w": w, "in_rows": rows, "in_cols": cols,
              "in_ident": ident}

    nc = bacc.Bacc("TRN2", target_bir_lowering=False, num_devices=1)
    aps = [nc.dram_tensor(k, a.shape, mybir.dt.from_np(a.dtype), kind="ExternalInput").ap()
           for k, a in arrays.items()]
    out = nc.dram_tensor("out", (B, N, D), FP32, kind="ExternalOutput").ap()
    two_layers(nc, *aps, out)
    r = run_bass_kernel_spmd(nc, [arrays], core_ids=[0])
    return r.results[0]["out"]
```

```python
from contextlib import ExitStack

import numpy as np
import concourse.bass as bass
from concourse import mybir

FP32 = mybir.dt.float32
F32R = mybir.dt.float32r
I32 = mybir.dt.int32
ALU = mybir.AluOpType
ACT = mybir.ActivationFunctionType

B, N, D, H = 64, 128, 256, 8
HD = D // H
G = 4
C = D // 128
T = 2 * N
PAIRS = B // 2
NUM_HOP = 4
ALPHA = 0.1
LN_EPS = 1e-05
SCALE = 1.0 / float(np.sqrt(HD))
MASKED = -1.0e30
BIG = 3.0e38
SPARE = 2


class Pair:

    def __init__(self, i, c):
        self.i, self.c = i, c

    def __add__(self, d):
        return Pair(self.i, self.c + d)

    def __sub__(self, d):
        return Pair(self.i, self.c - d)

    @property
    def parity(self):
        return self.c % 2

    @property
    def half(self):
        return self.i + self.c // 2

    @property
    def number(self):
        return self.i * 2 + self.c


class Count:

    def __init__(self, sem, per):
        self.sem, self.per = sem, per

    def at(self, pair, j=None):
        j = self.per if j is None else j
        return pair.i * (2 * self.per) + self.per * (pair.c + SPARE) + j


class DmaCount:

    def __init__(self, sems, dmas):
        self.sems, self.per = sems, 16 * dmas

    def sem(self, pair):
        return self.sems[pair.parity]

    def at(self, pair):
        return pair.half * self.per + 2 * self.per


def two_layers(nc, x, x_t, adj, w, rows, cols, ident_d, out):
    ctx = ExitStack()
    with ctx:
        def sb(name, shape, dt=FP32):
            return ctx.enter_context(nc.sbuf_tensor(name, shape, dt))

        def bank(name, n=1):
            return ctx.enter_context(nc.psum_tensor(name, [128, 512 * n], FP32))

        owned = {}

        def count(name, per=1, by=None):
            c = Count(ctx.enter_context(nc.semaphore(name)), per)
            owned.setdefault(by, []).append(c)
            return c

        def sem(name):
            return ctx.enter_context(nc.semaphore(name))

        NW = 7
        w_raw = sb("w_raw", [128, NW, C, D])
        w_hi = sb("w_hi", [128, NW, C, D], F32R)
        w_lo = sb("w_lo", [128, NW, C, D], F32R)
        row = sb("row", [128, 7, D])
        col = sb("col", [128, 4, C])
        bq0s = sb("bq0s", [128, C])
        ident = sb("ident", [128, 128])
        mhalf = sb("mhalf", [128, 2])
        BV0, BO0, GA0, BE0, BV1, GA1, BE1 = range(7)

        xt_in = [sb(f"xt_in{i}", [128, C, T]) for i in range(2)]
        x_in = [sb(f"x_in{i}", [128, 2, D]) for i in range(2)]
        adj_in = [sb(f"adj_in{i}", [128, 2, N], I32) for i in range(2)]
        mask = [sb(f"mask{i}", [128, 2, N]) for i in range(2)]

        xh = [sb(f"xh{l}", [128, C, T], F32R) for l in range(2)]
        xl = [sb(f"xl{l}", [128, C, T], F32R) for l in range(2)]
        qT = [sb(f"qT{l}", [128, C, T]) for l in range(2)]
        kT = [sb(f"kT{l}", [128, C, T]) for l in range(2)]
        v = [sb(f"v{l}", [128, 2, D]) for l in range(2)]
        sm = [sb(f"sm{l}", [128, 2, H, N]) for l in range(2)]
        nmax = [sb(f"nmax{l}", [128, 2, H]) for l in range(2)]
        ex = [sb(f"ex{l}", [128, 2, H, N]) for l in range(2)]
        tot = [sb(f"tot{l}", [128, 2, H]) for l in range(2)]
        rec = [sb(f"rec{l}", [128, 2, H]) for l in range(2)]
        pr = [sb(f"pr{l}", [128, 2, H, N]) for l in range(2)]
        pT = [sb(f"pT{l}", [128, 2, H, N]) for l in range(2)]
        bst = [sb(f"bst{l}", [128, 2, 6]) for l in range(2)]
        mv = [sb(f"mv{l}", [128, 2, 2]) for l in range(2)]
        ve = [sb(f"ve{l}", [128, 2]) for l in range(2)]
        rstd = [sb(f"rstd{l}", [128, 2]) for l in range(2)]
        y = [sb(f"y{l}", [128, 2, D]) for l in range(2)]
        yn = [sb(f"yn{l}", [128, 2, D]) for l in range(2)]
        yg = [sb(f"yg{l}", [128, 2, D]) for l in range(2)]
        oh = sb("oh", [128, 2 * C, N], F32R)
        ol = sb("ol", [128, 2 * C, N], F32R)
        xb = sb("xb", [128, 2, D])
        x1 = [sb(f"x1_{i}", [128, 2, D]) for i in range(2)]
        z0s = sb("z0s", [128, 2, D])
        zf = sb("zf", [128, 2, D])
        hT = sb("hT", [128, 2, C, N])
        z = sb("z", [128, 2, D])
        o_t = [sb(f"o_t{i}", [128, 2, D]) for i in range(2)]

        psS = bank("psS", 4)
        psT = [bank(f"psT{i}") for i in range(2)]
        psM = [bank(f"psM{i}") for i in range(2)]

        qr = [count(f"q{l}_ready", 1, "pe") for l in range(2)]
        kr = [count(f"k{l}_ready", 1, "pe") for l in range(2)]
        vr = [count(f"v{l}_ready", 1, "pe") for l in range(2)]
        sr = [count(f"s{l}_ready", 1, "pe") for l in range(2)]
        tr = [count(f"pT{l}_ready", 4, "pe") for l in range(2)]
        avr = count("av_ready", 1, "pe")
        wor = count("wo_ready", 1, "pe")
        x1r = count("x1T_ready", 1, "pe")
        hr = count("hopT_ready", NUM_HOP, "pe")
        zr = count("hop_ready", NUM_HOP, "pe")

        q_s = [count(f"q{l}_saved", 1, "act") for l in range(2)]
        exps = [count(f"exp{l}_done", 2, "act") for l in range(2)]
        pT_s = [count(f"pT{l}_saved", 4, "act") for l in range(2)]
        oh_s = count("oh_saved", 1, "act")
        x1h_s = count("x1h_saved", 1, "act")
        hT_s = count("hopT_saved", NUM_HOP, "act")

        k_s = [count(f"k{l}_saved", 1, "dve") for l in range(2)]
        v_s = [count(f"v{l}_saved", 1, "dve") for l in range(2)]
        mx = [count(f"masked{l}_done", 4, "dve") for l in range(2)]
        rec_s = [count(f"rec{l}_done", 2, "dve") for l in range(2)]
        tmp_s = count("rec1_raw_done", 2, "dve")
        xh_s = count("xh_saved", 1, "dve")
        xl_s = count("xl_saved", 1, "dve")
        mask_s = count("mask_done", 1, "dve")
        ol_s = count("ol_saved", 1, "dve")
        y_s = count("y0_saved", 1, "dve")
        bn_s = [count(f"bn{l}_done", 1, "dve") for l in range(2)]
        ag_s = [count(f"aggr{l}_done", 1, "dve") for l in range(2)]
        ve_s = [count(f"var_eps{l}_done", 1, "dve") for l in range(2)]
        yn_s = [count(f"normed{l}_done", 1, "dve") for l in range(2)]
        yg_s = count("gamma0_done", 1, "dve")
        x1_s = count("x1_done", 1, "dve")
        x1l_s = count("x1l_saved", 1, "dve")
        z_s = count("hop_saved", NUM_HOP, "dve")

        xb_s = count("xb_done", 1, "pool")
        pr_s = [count(f"probs{l}_done", 2, "pool") for l in range(2)]
        rstd_s = [count(f"rstd{l}_done", 1, "pool") for l in range(2)]
        z0_s = count("z0s_done", 1, "pool")
        zf_s = count("zf_done", 1, "pool")
        g1_s = count("gamma1_done", 1, "pool")
        o_s = count("out_done", 1, "pool")

        in_s = DmaCount([sem("in_even"), sem("in_odd")], 3)
        st_s = DmaCount([sem("store_even"), sem("store_odd")], 1)
        w_in = [sem(f"w_in{i}") for i in range(NW)]
        c_in = sem("const_in")
        wh_s = sem("w_hi_done")
        wl_s = sem("w_lo_done")
        bq_s = sem("bq0s_done")
        mh_s = sem("mhalf_done")
        own = sem("own_instruction")

        block = ctx.enter_context(nc.Block())

        def credit(eng, who):
            for c in owned[who]:
                eng.sem_inc(c.sem, c.per * SPARE)

        def pipeline(eng, step, peel=0):
            step(Pair(0, -1), False, False, True)
            step(Pair(0, 0), False, True, True)
            turns = (PAIRS - 2) // 2 - peel
            with eng.Fori(0, turns) as i:
                for u in range(2):
                    step(Pair(i, 1 + u), True, True, True)
            for t in range(1 + 2 * turns, PAIRS - 1):
                step(Pair(0, t), True, True, True)
            step(Pair(0, PAIRS - 1), True, True, False)
            step(Pair(0, PAIRS), True, False, False)

        def both(row_i):
            return row[:, row_i:row_i + 1, :].broadcast_to([128, 2, D])

        @block.sync
        def _(sp):
            for s in st_s.sems:
                sp.sem_inc(s, 16)
            for s in in_s.sems:
                sp.sem_inc(s, in_s.per)

            def load(p):
                sp.wait_ge(xl_s.sem, xl_s.at(p - 2))
                sp.wait_ge(xb_s.sem, xb_s.at(p - 2))
                sp.wait_ge(mask_s.sem, mask_s.at(p - 2))
                i = p.parity
                sp.dma_start(xt_in[i][:, :, :], x_t[bass.ds(p.number, 1)].rearrange("a p c t -> (a p) c t")
                             ).then_inc(in_s.sem(p), 16)
                sp.dma_start(adj_in[i][:, :, :], adj[bass.ds(p.number * 2, 2)].rearrange("b n m -> n b m")
                             ).then_inc(in_s.sem(p), 16)
                sp.dma_start(x_in[i][:, :, :], x[bass.ds(p.number * 2, 2)].rearrange("b n d -> n b d")
                             ).then_inc(in_s.sem(p), 16)

            load(Pair(0, 0))
            for i in range(NW):
                if i == 3:
                    sp.dma_start(col[:, :, :], cols).then_inc(c_in, 16)
                    sp.dma_start(row[:, :, :], rows.partition_broadcast(128)).then_inc(c_in, 16)
                    sp.dma_start(ident[:, :], ident_d).then_inc(c_in, 16)
                sp.dma_start(w_raw[:, i, :, :], w[i].rearrange("(c p) o -> p c o", p=128)).then_inc(w_in[i], 16)
            load(Pair(0, 1))

            def step(t, layer1, finish0, start0):
                if start0 and not (isinstance(t.i, int) and (t.c < 0 or t.c + 2 >= PAIRS)):
                    load(t + 2)
                if layer1:
                    p = t - 1
                    sp.wait_ge(o_s.sem, o_s.at(p))
                    sp.dma_start(out[bass.ds(p.number * 2, 2)].rearrange("b n d -> n b d"), o_t[p.parity][:, :, :]
                                 ).then_inc(st_s.sem(p), 16)

            pipeline(sp, step, peel=1)
            for p in (Pair(0, PAIRS - 2), Pair(0, PAIRS - 1)):
                sp.wait_ge(st_s.sem(p), st_s.at(p))

        @block.tensor
        def _(pe):
            credit(pe, "pe")
            parts = ((0, 0), (1, 0), (0, 1))

            def project_T(l, wi, dst, done):
                x_p, w_p = (xh[l], xl[l]), (w_hi, w_lo)
                for c in range(C):
                    for n, (a, e) in enumerate(parts):
                        for kc in range(C):
                            last = nc.tensor.matmul(dst[:, c * T:(c + 1) * T],
                                                    w_p[e][:, wi, kc, c * 128:(c + 1) * 128],
                                                    x_p[a][:, kc, :], start=(n == 0 and kc == 0),
                                                    stop=(n == 2 and kc == C - 1))
                last.then_inc(done.sem, 1)

            def project(x_p, b, wi, dst, done):
                w_p = (w_hi, w_lo)
                for n, (a, e) in enumerate(parts):
                    for kc in range(C):
                        last = nc.tensor.matmul(dst[:, b * D:(b + 1) * D], x_p[a](kc), w_p[e][:, wi, kc, :],
                                                start=(n == 0 and kc == 0), stop=(n == 2 and kc == C - 1))
                if b:
                    last.then_inc(done.sem, 1)

            def values(l, b, dst):
                project([lambda kc, m=m: m[:, kc, b * N:(b + 1) * N] for m in (xh[l], xl[l])], b,
                        (2, 6)[l], dst, vr[l])

            def scores(l, b, c):
                for g in range(G):
                    r = slice(32 * g, 32 * g + 32)
                    o = 512 * g + (b * C + c) * N
                    last = nc.tensor.matmul(psS[:, o:o + N], qT[l][r, c, b * N:(b + 1) * N],
                                            kT[l][r, c, b * N:(b + 1) * N], start=True, stop=True)
                if b and c == C - 1:
                    last.then_inc(sr[l].sem, 1)

            def turn_probs(l, b, c):
                for g in range(G):
                    last = nc.tensor.transpose(psT[c][:, g * N:(g + 1) * N], pr[l][:, b, G * c + g, :], ident[:, :])
                last.then_inc(tr[l].sem, 1)

            def spread(l, src, dst, done):
                for b in range(2):
                    for c in range(C):
                        for g in range(G):
                            h, o = G * c + g, (b * C + c) * N
                            last = nc.tensor.matmul(dst[32 * g:32 * g + 32, o:o + N],
                                                    src[:, b, h * HD:(h + 1) * HD], pT[l][:, b, h, :],
                                                    start=True, stop=True)
                last.then_inc(done.sem, 1)

            def hop(p, j):
                if j:
                    pe.wait_ge(z_s.sem, z_s.at(p, j))
                spread(1, z if j else v[1], psT[0], hr)

            def turn_hop(p, j):
                pe.wait_ge(hT_s.sem, hT_s.at(p, j + 1))
                for b in range(2):
                    for c in range(C):
                        o = b * D + c * 128
                        last = nc.tensor.transpose(psT[1][:, o:o + 128], hT[:, b, c, :], ident[:, :])
                last.then_inc(zr.sem, 1)

            def step(t, layer1, finish0, start0):
                p, n = t - 1, t + 1
                if finish0:
                    pe.wait_ge(z_s.sem, z_s.at(p - 1))
                    for b in range(2):
                        pe.wait_ge(pr_s[0].sem, pr_s[0].at(t, b + 1))
                        for c in range(C):
                            if b:
                                pe.wait_ge(pT_s[0].sem, pT_s[0].at(t, c + 1))
                            turn_probs(0, b, c)
                    pe.wait_ge(v_s[0].sem, v_s[0].at(t))
                    pe.wait_ge(k_s[1].sem, k_s[1].at(p))
                    pe.wait_ge(pT_s[0].sem, pT_s[0].at(t))
                    spread(0, v[0], psM[0], avr)
                if start0:
                    if isinstance(t.i, int) and t.c < 0:
                        pe.wait_ge(wh_s, 3)
                        pe.wait_ge(wl_s, 3)
                    pe.wait_ge(xl_s.sem, xl_s.at(n))
                    pe.wait_ge(v_s[1].sem, v_s[1].at(p))
                    project_T(0, 0, psM[1], qr[0])
                    pe.wait_ge(ol_s.sem, ol_s.at(t))
                    project_T(0, 1, psM[0], kr[0])
                    pe.wait_ge(q_s[0].sem, q_s[0].at(n))
                if finish0:
                    if isinstance(t.i, int) and t.c == 0:
                        pe.wait_ge(wh_s, NW)
                        pe.wait_ge(wl_s, NW)
                    pe.wait_ge(ol_s.sem, ol_s.at(t))
                    pe.wait_ge(v_s[1].sem, v_s[1].at(p))
                    for b in range(2):
                        project([lambda c, m=m: m[:, b * C + c, :] for m in (oh, ol)], b, 3, psM[1], wor)
                if start0:
                    pe.wait_ge(k_s[0].sem, k_s[0].at(n))
                    pe.wait_ge(mx[1].sem, mx[1].at(p))
                    for b in range(2):
                        for c in range(C):
                            scores(0, b, c)
                if layer1:
                    for b in range(2):
                        pe.wait_ge(pr_s[1].sem, pr_s[1].at(p, b + 1))
                        for c in range(C):
                            if b:
                                pe.wait_ge(pT_s[1].sem, pT_s[1].at(p, c + 1))
                            turn_probs(1, b, c)
                    pe.wait_ge(pT_s[1].sem, pT_s[1].at(p))
                    hop(p, 0)
                if finish0:
                    pe.wait_ge(x1_s.sem, x1_s.at(t))
                    for kc in range(C):
                        for b in range(2):
                            o = kc * T + b * N
                            last = nc.tensor.transpose(psM[1][:, o:o + N], x1[t.parity][:, b, kc * 128:(kc + 1) * 128],
                                                       ident[:, :])
                    last.then_inc(x1r.sem, 1)
                if start0:
                    values(0, 0, psM[0])
                if layer1:
                    turn_hop(p, 0)
                if start0:
                    values(0, 1, psM[0])
                if layer1:
                    hop(p, 1)
                if finish0:
                    pe.wait_ge(x1l_s.sem, x1l_s.at(t))
                    project_T(1, 4, psM[1], qr[1])
                if layer1:
                    turn_hop(p, 1)
                if finish0:
                    if start0:
                        pe.wait_ge(v_s[0].sem, v_s[0].at(n))
                    project_T(1, 5, psM[0], kr[1])
                if layer1:
                    hop(p, 2)
                if finish0:
                    pe.wait_ge(q_s[1].sem, q_s[1].at(t))
                    values(1, 0, psM[1])
                    values(1, 1, psM[1])
                if layer1:
                    turn_hop(p, 2)
                if finish0:
                    pe.wait_ge(k_s[1].sem, k_s[1].at(t))
                    if start0:
                        pe.wait_ge(mx[0].sem, mx[0].at(n))
                    scores(1, 0, 0)
                if layer1:
                    hop(p, 3)
                if finish0:
                    scores(1, 0, 1)
                if layer1:
                    turn_hop(p, 3)
                if finish0:
                    scores(1, 1, 0)
                    scores(1, 1, 1)

            pe.wait_ge(c_in, 48)
            pipeline(pe, step)

        @block.scalar
        def _(act):
            credit(act, "act")
            for i in range(NW):
                act.wait_ge(w_in[i], 16)
                nc.scalar.activation(w_hi[:, i, :, :], w_raw[:, i, :, :], ACT.Copy).then_inc(wh_s, 1)
            act.wait_ge(c_in, 48)
            act.wait_ge(bq_s, 1)

            def save_q(l, p, ps):
                act.wait_ge(qr[l].sem, qr[l].at(p))
                act.wait_ge(sr[l].sem, sr[l].at(p - 1))
                for c in range(C):
                    b = bq0s[:, c:c + 1] if l == 0 else col[:, 2, c:c + 1]
                    last = nc.scalar.activation(qT[l][:, c, :], ps[:, c * T:(c + 1) * T], ACT.Identity, bias=b,
                                                scale=SCALE if l == 0 else 1.0)
                last.then_inc(q_s[l].sem, 1)

            def exp_head(l, p, b, h):
                if h == 0:
                    act.wait_ge(pr_s[l].sem, pr_s[l].at(p - 1, b + 1))
                if h % 4 == 0:
                    act.wait_ge(mx[l].sem, mx[l].at(p, 2 * b + h // 4 + 1))
                e = nc.scalar.activation(ex[l][:, b, h, :], sm[l][:, b, h, :], ACT.Exp, scale=-1.0,
                                         bias=nmax[l][:, b, h:h + 1], accum_out=tot[l][:, b, h:h + 1])
                if h == H - 1:
                    e.then_inc(exps[l].sem, 1)

            def save_pT(l, p, b, c):
                act.wait_ge(tr[l].sem, tr[l].at(p, 2 * b + c + 1))
                nc.scalar.activation(pT[l][:, b, G * c:G * c + G, :],
                                     psT[c][:, :].rearrange("p (g n) -> p g n", g=G), ACT.Copy
                                     ).then_inc(pT_s[l].sem, 1)

            def save_hop(p, j):
                act.wait_ge(hr.sem, hr.at(p, j + 1))
                if j:
                    act.wait_ge(zr.sem, zr.at(p, j))
                else:
                    act.wait_ge(zr.sem, zr.at(p - 1))
                nc.scalar.activation(hT[:, :, :, :], psT[0][:, :].rearrange("p (b c n) -> p b c n", b=2, c=C),
                                     ACT.Copy).then_inc(hT_s.sem, 1)

            def step(t, layer1, finish0, start0):
                p, n = t - 1, t + 1

                def some_exps(l, pair, there, first, end):
                    if there:
                        for k in range(first, end):
                            exp_head(l, pair, k // H, k % H)

                if finish0:
                    act.wait_ge(avr.sem, avr.at(t - 1))
                    for b in range(2):
                        for c in range(C):
                            save_pT(0, t, b, c)
                some_exps(1, p, layer1, 0, 3)
                if finish0:
                    act.wait_ge(avr.sem, avr.at(t))
                    act.wait_ge(wor.sem, wor.at(t - 1))
                    nc.scalar.activation(oh[:, :, :], psM[0][:, :].rearrange("p (a n) -> p a n", n=N), ACT.Copy
                                         ).then_inc(oh_s.sem, 1)
                some_exps(1, p, layer1, 3, 5)
                if start0:
                    save_q(0, n, psM[1])
                some_exps(1, p, layer1, 5, 16)
                if layer1:
                    act.wait_ge(hr.sem, hr.at(p - 1))
                    for b in range(2):
                        for c in range(C):
                            save_pT(1, p, b, c)
                some_exps(0, n, start0, 0, 1)
                if layer1:
                    save_hop(p, 0)
                if finish0:
                    act.wait_ge(x1r.sem, x1r.at(t))
                    act.wait_ge(vr[1].sem, vr[1].at(t - 1))
                    nc.scalar.activation(xh[1][:, :, :], psM[1][:, :].rearrange("p (c t) -> p c t", c=C), ACT.Copy
                                         ).then_inc(x1h_s.sem, 1)
                some_exps(0, n, start0, 1, 6)
                if layer1:
                    save_hop(p, 1)
                some_exps(0, n, start0, 6, 8)
                if finish0:
                    save_q(1, t, psM[1])
                some_exps(0, n, start0, 8, 12)
                if layer1:
                    save_hop(p, 2)
                some_exps(0, n, start0, 12, 16)
                if layer1:
                    save_hop(p, 3)

            pipeline(act, step)

        @block.vector
        def _(dve):
            credit(dve, "dve")
            dve.wait_ge(c_in, 48)
            nc.vector.tensor_scalar(bq0s[:, :], col[:, 0, :], SCALE, None, ALU.mult).then_inc(bq_s, 1)

            def split_w(i):
                dve.wait_ge(wh_s, i + 1)
                nc.vector.tensor_tensor(w_lo[:, i, :, :], w_raw[:, i, :, :], w_hi[:, i, :, :].bitcast(FP32), ALU.subtract
                                        ).then_inc(wl_s, 1)

            def split_x(p):
                dve.wait_ge(in_s.sem(p), in_s.at(p))
                dve.wait_ge(vr[0].sem, vr[0].at(p - 1))
                nc.vector.tensor_copy(xh[0][:, :, :], xt_in[p.parity][:, :, :]).then_inc(xh_s.sem, 1)
                dve.wait_ge(xh_s.sem, xh_s.at(p))
                nc.vector.tensor_tensor(xl[0][:, :, :], xt_in[p.parity][:, :, :], xh[0][:, :, :].bitcast(FP32),
                                        ALU.subtract).then_inc(xl_s.sem, 1)

            def make_mask(p):
                dve.wait_ge(mx[1].sem, mx[1].at(p - 2))
                nc.vector.tensor_scalar(mask[p.parity][:, :, :], adj_in[p.parity][:, :, :], 0.0, MASKED,
                                        ALU.is_equal, ALU.mult).then_inc(mask_s.sem, 1)

            def save_k(l, p, ps):
                dve.wait_ge(kr[l].sem, kr[l].at(p))
                dve.wait_ge(sr[l].sem, sr[l].at(p - 1))
                for c in range(C):
                    last = nc.vector.tensor_scalar(kT[l][:, c, :], ps[:, c * T:(c + 1) * T],
                                                   col[:, 2 * l + 1, c:c + 1], None, ALU.add)
                last.then_inc(k_s[l].sem, 1)

            def save_v(l, p, ps):
                dve.wait_ge(vr[l].sem, vr[l].at(p))
                if l == 0:
                    dve.wait_ge(avr.sem, avr.at(p - 1))
                else:
                    dve.wait_ge(hr.sem, hr.at(p - 1, 1))
                    dve.wait_ge(z0_s.sem, z0_s.at(p - 1))
                nc.vector.tensor_tensor(v[l][:, :, :], ps[:, :].rearrange("p (b d) -> p b d", b=2),
                                        both(BV1 if l else BV0), ALU.add).then_inc(v_s[l].sem, 1)

            def mask_scores(l, p, b):
                if b == 0:
                    dve.wait_ge(sr[l].sem, sr[l].at(p))
                    dve.wait_ge(mask_s.sem, mask_s.at(p))
                    dve.wait_ge(exps[l].sem, exps[l].at(p - 1))
                    dve.sem_inc(own, 1)
                for c in range(C):
                    for g in range(G):
                        h, o = G * c + g, 512 * g + (b * C + c) * N
                        last = nc.vector.tensor_tensor_reduce(
                            sm[l][:, b, h, :], psS[:, o:o + N], mask[p.parity][:, b, :], -1.0, BIG,
                            ALU.add, ALU.min, nmax[l][:, b, h:h + 1])
                    last.then_inc(mx[l].sem, 1)

            def reciprocals(l, p, b):
                dve.wait_ge(exps[l].sem, exps[l].at(p, b + 1))
                dve.wait_ge(pr_s[l].sem, pr_s[l].at(p - 1, b + 1))
                r = nc.vector.reciprocal(rec[l][:, b, :], tot[l][:, b, :])
                if l:
                    r.then_inc(tmp_s.sem, 1)
                    dve.wait_ge(tmp_s.sem, tmp_s.at(p, b + 1))
                    r = nc.vector.tensor_scalar(rec[l][:, b, :], rec[l][:, b, :], 1.0 - ALPHA, None, ALU.mult)
                r.then_inc(rec_s[l].sem, 1)

            def statistics(l, p):
                for b in range(2):
                    last = nc.vector.bn_stats(bst[l][:, b, :], y[l][:, b, :])
                last.then_inc(bn_s[l].sem, 1)
                dve.wait_ge(bn_s[l].sem, bn_s[l].at(p))
                dve.sem_inc(own, 1)
                for b in range(2):
                    last = nc.vector.bn_aggr(mv[l][:, b, :], bst[l][:, b, :])
                last.then_inc(ag_s[l].sem, 1)
                dve.wait_ge(ag_s[l].sem, ag_s[l].at(p))
                dve.wait_ge(rstd_s[l].sem, rstd_s[l].at(p - 1))
                nc.vector.tensor_scalar(ve[l][:, :], mv[l][:, :, 1], LN_EPS, None, ALU.add).then_inc(ve_s[l].sem, 1)

            def normalise(l, p):
                dve.wait_ge(rstd_s[l].sem, rstd_s[l].at(p))
                if l:
                    dve.wait_ge(g1_s.sem, g1_s.at(p - 1))
                for b in range(2):
                    last = nc.vector.tensor_scalar(yn[l][:, b, :], y[l][:, b, :], mv[l][:, b, 0:1], rstd[l][:, b:b + 1],
                                                   ALU.subtract, ALU.mult)
                last.then_inc(yn_s[l].sem, 1)

            def add_hop(p, j):
                dve.wait_ge(zr.sem, zr.at(p, j + 1))
                end = j == NUM_HOP - 1
                nc.vector.tensor_tensor((y[1] if end else z)[:, :, :], psT[1][:, :].rearrange("p (b d) -> p b d", b=2),
                                        (zf if end else z0s)[:, :, :], ALU.add).then_inc(z_s.sem, 1)

            def step(t, layer1, finish0, start0):
                p, n = t - 1, t + 1
                if start0 and not (isinstance(t.i, int) and t.c < 0):
                    split_x(n)
                if layer1:
                    mask_scores(1, p, 0)
                if finish0:
                    dve.wait_ge(oh_s.sem, oh_s.at(t))
                    dve.wait_ge(wor.sem, wor.at(t - 1))
                    nc.vector.tensor_tensor(ol[:, :, :], psM[0][:, :].rearrange("p (a n) -> p a n", n=N),
                                            oh[:, :, :].bitcast(FP32), ALU.subtract).then_inc(ol_s.sem, 1)
                if layer1:
                    mask_scores(1, p, 1)
                if start0:
                    if not (isinstance(t.i, int) and t.c < 0):
                        make_mask(n)
                    save_k(0, n, psM[0])
                if layer1:
                    reciprocals(1, p, 0)
                if finish0:
                    dve.wait_ge(wor.sem, wor.at(t))
                    dve.wait_ge(xb_s.sem, xb_s.at(t))
                    nc.vector.tensor_tensor(y[0][:, :, :], psM[1][:, :].rearrange("p (b d) -> p b d", b=2), xb[:, :, :],
                                            ALU.add).then_inc(y_s.sem, 1)
                    dve.wait_ge(y_s.sem, y_s.at(t))
                    statistics(0, t)
                if layer1:
                    reciprocals(1, p, 1)
                if finish0:
                    normalise(0, t)
                    dve.wait_ge(yn_s[0].sem, yn_s[0].at(t))
                    nc.vector.tensor_tensor(yg[0][:, :, :], yn[0][:, :, :], both(GA0), ALU.mult).then_inc(yg_s.sem, 1)
                    dve.wait_ge(yg_s.sem, yg_s.at(t))
                    dve.wait_ge(x1r.sem, x1r.at(t - 2))
                    dve.wait_ge(zf_s.sem, zf_s.at(t - 2))
                    nc.vector.tensor_tensor(x1[t.parity][:, :, :], yg[0][:, :, :], both(BE0), ALU.add
                                            ).then_inc(x1_s.sem, 1)
                if start0:
                    mask_scores(0, n, 0)
                    mask_scores(0, n, 1)
                if finish0:
                    dve.wait_ge(x1h_s.sem, x1h_s.at(t))
                    nc.vector.tensor_tensor(xl[1][:, :, :], psM[1][:, :].rearrange("p (c t) -> p c t", c=C),
                                            xh[1][:, :, :].bitcast(FP32), ALU.subtract).then_inc(x1l_s.sem, 1)
                if layer1:
                    dve.wait_ge(zf_s.sem, zf_s.at(p))
                    add_hop(p, 0)
                if start0:
                    save_v(0, n, psM[0])
                if layer1:
                    add_hop(p, 1)
                if finish0:
                    save_k(1, t, psM[0])
                if start0:
                    reciprocals(0, n, 0)
                if finish0:
                    save_v(1, t, psM[1])
                if layer1:
                    add_hop(p, 2)
                if start0:
                    reciprocals(0, n, 1)
                if layer1:
                    add_hop(p, 3)
                    dve.wait_ge(z_s.sem, z_s.at(p))
                    statistics(1, p)
                    normalise(1, p)

            for i in range(4):
                split_w(i)
            split_x(Pair(0, 0))
            make_mask(Pair(0, 0))
            for i in range(4, NW):
                split_w(i)

            pipeline(dve, step)

        @block.gpsimd
        def _(pool):
            credit(pool, "pool")
            nc.gpsimd.memset(mhalf[:, :], -0.5).then_inc(mh_s, 1)
            pool.wait_ge(mh_s, 1)
            pool.wait_ge(c_in, 48)

            def probabilities(l, p, b):
                pool.wait_ge(rec_s[l].sem, rec_s[l].at(p, b + 1))
                pool.wait_ge(tr[l].sem, tr[l].at(p - 1, 2 * b + 2))
                nc.gpsimd.tensor_tensor(pr[l][:, b, :, :], ex[l][:, b, :, :],
                                        rec[l][:, b, :].unsqueeze(2).broadcast_to([128, H, N]), ALU.mult
                                        ).then_inc(pr_s[l].sem, 1)

            def inverse_root(l, p):
                pool.wait_ge(ve_s[l].sem, ve_s[l].at(p))
                pool.wait_ge(yn_s[l].sem, yn_s[l].at(p - 1))
                nc.gpsimd.tensor_tensor(rstd[l][:, :], ve[l][:, :], mhalf[:, :], ALU.pow).then_inc(rstd_s[l].sem, 1)

            def step(t, layer1, finish0, start0):
                p, n = t - 1, t + 1
                if finish0:
                    pool.wait_ge(in_s.sem(t), in_s.at(t))
                    pool.wait_ge(y_s.sem, y_s.at(t - 1))
                    nc.gpsimd.tensor_tensor(xb[:, :, :], x_in[t.parity][:, :, :], both(BO0), ALU.add
                                            ).then_inc(xb_s.sem, 1)
                if layer1:
                    pool.wait_ge(v_s[1].sem, v_s[1].at(p))
                    pool.wait_ge(z_s.sem, z_s.at(p - 1))
                    pool.sem_inc(own, 1)
                    nc.gpsimd.tensor_scalar(z0s[:, :, :], v[1][:, :, :], ALPHA, 0.0, ALU.mult, ALU.add
                                            ).then_inc(z0_s.sem, 1)
                    pool.wait_ge(z0_s.sem, z0_s.at(p))
                    pool.wait_ge(x1_s.sem, x1_s.at(p))
                    nc.gpsimd.tensor_tensor(zf[:, :, :], z0s[:, :, :], x1[p.parity][:, :, :], ALU.add
                                            ).then_inc(zf_s.sem, 1)
                    probabilities(1, p, 0)
                if finish0:
                    inverse_root(0, t)
                if layer1:
                    probabilities(1, p, 1)
                if start0:
                    probabilities(0, n, 0)
                    probabilities(0, n, 1)
                if layer1:
                    inverse_root(1, p)
                if layer1:
                    pool.wait_ge(yn_s[1].sem, yn_s[1].at(p))
                    nc.gpsimd.tensor_tensor(yg[1][:, :, :], yn[1][:, :, :], both(GA1), ALU.mult).then_inc(g1_s.sem, 1)
                    pool.wait_ge(g1_s.sem, g1_s.at(p))
                    pool.wait_ge(st_s.sem(p), st_s.at(p - 2))
                    nc.gpsimd.tensor_tensor(o_t[p.parity][:, :, :], yg[1][:, :, :], both(BE1), ALU.add
                                            ).then_inc(o_s.sem, 1)

            pipeline(pool, step)


def kernel(**inputs):
    from concourse import bacc
    from concourse.bass_utils import run_bass_kernel_spmd

    def arr(name):
        return np.ascontiguousarray(inputs[name])

    x = arr("x")
    x_t = np.ascontiguousarray(x.reshape(PAIRS, T, C, 128).transpose(0, 3, 2, 1))
    w = np.stack([arr("L0_gnn_Wq"), arr("L0_gnn_Wk"), arr("L0_gnn_Wv"), arr("L0_gnn_Wo"),
                  arr("L1_gnn_Wq").T, arr("L1_gnn_Wk").T, arr("L1_gnn_Wv").T])
    rows = np.stack([arr(n) for n in ("L0_gnn_bv", "L0_gnn_bo", "L0_gnn_gamma", "L0_gnn_beta",
                                      "L1_gnn_bv", "L1_gnn_gamma", "L1_gnn_beta")])
    cols = np.ascontiguousarray(np.stack([arr(n).reshape(C, 128) for n in (
        "L0_gnn_bq", "L0_gnn_bk", "L1_gnn_bq", "L1_gnn_bk")]).transpose(2, 0, 1))
    ident = np.eye(128, dtype=np.float32)
    arrays = {"in_x": x, "in_x_t": x_t, "in_adj": arr("adj"), "in_w": w, "in_rows": rows, "in_cols": cols,
              "in_ident": ident}

    nc = bacc.Bacc("TRN2", target_bir_lowering=False, num_devices=1)
    aps = [nc.dram_tensor(k, a.shape, mybir.dt.from_np(a.dtype), kind="ExternalInput").ap()
           for k, a in arrays.items()]
    out = nc.dram_tensor("out", (B, N, D), FP32, kind="ExternalOutput").ap()
    two_layers(nc, *aps, out)
    r = run_bass_kernel_spmd(nc, [arrays], core_ids=[0])
    return r.results[0]["out"]
```

```python
from contextlib import ExitStack

import numpy as np
import concourse.bass as bass
from concourse import mybir

FP32 = mybir.dt.float32
F32R = mybir.dt.float32r
I32 = mybir.dt.int32
ALU = mybir.AluOpType
ACT = mybir.ActivationFunctionType

B, N, D, H = 64, 128, 256, 8
HD = D // H
G = 4
C = D // 128
T = 2 * N
PAIRS = B // 2
NUM_HOP = 4
ALPHA = 0.1
LN_EPS = 1e-05
SCALE = 1.0 / float(np.sqrt(HD))
MASKED = -1.0e30
BIG = 3.0e38
SPARE = 2


class Pair:

    def __init__(self, i, c):
        self.i, self.c = i, c

    def __add__(self, d):
        return Pair(self.i, self.c + d)

    def __sub__(self, d):
        return Pair(self.i, self.c - d)

    @property
    def parity(self):
        return self.c % 2

    @property
    def half(self):
        return self.i + self.c // 2

    @property
    def number(self):
        return self.i * 2 + self.c


class Count:

    def __init__(self, sem, per):
        self.sem, self.per = sem, per

    def at(self, pair, j=None):
        j = self.per if j is None else j
        return pair.i * (2 * self.per) + self.per * (pair.c + SPARE) + j


class DmaCount:

    def __init__(self, sems, dmas):
        self.sems, self.per = sems, 16 * dmas

    def sem(self, pair):
        return self.sems[pair.parity]

    def at(self, pair):
        return pair.half * self.per + 2 * self.per


def two_layers(nc, x, x_t, adj, w, rows, cols, ident_d, out):
    ctx = ExitStack()
    with ctx:
        def sb(name, shape, dt=FP32):
            return ctx.enter_context(nc.sbuf_tensor(name, shape, dt))

        def bank(name, n=1):
            return ctx.enter_context(nc.psum_tensor(name, [128, 512 * n], FP32))

        P0, P1 = Pair(0, 0), Pair(0, 1)
        Q, R = Pair(0, PAIRS - 2), Pair(0, PAIRS - 1)
        owned = {}

        def count(name, per=1, by=None):
            c = Count(ctx.enter_context(nc.semaphore(name)), per)
            owned.setdefault(by, []).append(c)
            return c

        def sem(name):
            return ctx.enter_context(nc.semaphore(name))

        NW = 7
        w_raw = sb("w_raw", [128, NW, C, D])
        w_hi = sb("w_hi", [128, NW, C, D], F32R)
        w_lo = sb("w_lo", [128, NW, C, D], F32R)
        row = sb("row", [128, 7, D])
        col = sb("col", [128, 4, C])
        bq0s = sb("bq0s", [128, C])
        ident = sb("ident", [128, 128])
        mhalf = sb("mhalf", [128, 2])
        BV0, BO0, GA0, BE0, BV1, GA1, BE1 = range(7)

        xt_in = [sb(f"xt_in{i}", [128, C, T]) for i in range(2)]
        x_in = [sb(f"x_in{i}", [128, 2, D]) for i in range(2)]
        adj_in = [sb(f"adj_in{i}", [128, 2, N], I32) for i in range(2)]
        mask = [sb(f"mask{i}", [128, 2, N]) for i in range(2)]

        xh = [sb(f"xh{l}", [128, C, T], F32R) for l in range(2)]
        xl = [sb(f"xl{l}", [128, C, T], F32R) for l in range(2)]
        qT = [sb(f"qT{l}", [128, C, T]) for l in range(2)]
        kT = [sb(f"kT{l}", [128, C, T]) for l in range(2)]
        v = [sb(f"v{l}", [128, 2, D]) for l in range(2)]
        sm = [sb(f"sm{l}", [128, 2, H, N]) for l in range(2)]
        nmax = [sb(f"nmax{l}", [128, 2, H]) for l in range(2)]
        ex = [sb(f"ex{l}", [128, 2, H, N]) for l in range(2)]
        tot = [sb(f"tot{l}", [128, 2, H]) for l in range(2)]
        rec = [sb(f"rec{l}", [128, 2, H]) for l in range(2)]
        pr = [sb(f"pr{l}", [128, 2, H, N]) for l in range(2)]
        pT = [sb(f"pT{l}", [128, 2, H, N]) for l in range(2)]
        bst = [sb(f"bst{l}", [128, 2, 6]) for l in range(2)]
        mv = [sb(f"mv{l}", [128, 2, 2]) for l in range(2)]
        ve = [sb(f"ve{l}", [128, 2]) for l in range(2)]
        rstd = [sb(f"rstd{l}", [128, 2]) for l in range(2)]
        y = [sb(f"y{l}", [128, 2, D]) for l in range(2)]
        yg = [sb(f"yg{l}", [128, 2, D]) for l in range(2)]
        oh = sb("oh", [128, 2 * C, N], F32R)
        ol = sb("ol", [128, 2 * C, N], F32R)
        xb = sb("xb", [128, 2, D])
        x1 = [sb(f"x1_{i}", [128, 2, D]) for i in range(2)]
        z0s = sb("z0s", [128, 2, D])
        zf = sb("zf", [128, 2, D])
        hT = sb("hT", [128, 2, C, N])
        z = sb("z", [128, 2, D])
        o_t = [sb(f"o_t{i}", [128, 2, D]) for i in range(2)]

        psS = bank("psS", 4)
        psT = [bank(f"psT{i}") for i in range(2)]
        psM = [bank(f"psM{i}") for i in range(2)]
        turned = [[psM[0], psT[0]], psT]
        last_hopT, last_hop = [psT[0], psM[0]], [psT[1], psM[1]]

        qr = [count(f"q{l}_ready", 1, "pe") for l in range(2)]
        kr = [count(f"k{l}_ready", 1, "pe") for l in range(2)]
        vr = [count(f"v{l}_ready", 1, "pe") for l in range(2)]
        sr = [count(f"s{l}_ready", 1, "pe") for l in range(2)]
        tr = [count(f"pT{l}_ready", 4, "pe") for l in range(2)]
        avr = count("av_ready", 1, "pe")
        wor = count("wo_ready", 1, "pe")
        x1r = count("x1T_ready", 1, "pe")
        hr = count("hopT_ready", NUM_HOP, "pe")
        zr = count("hop_ready", NUM_HOP, "pe")

        q_s = [count(f"q{l}_saved", 1, "act") for l in range(2)]
        exps = [count(f"exp{l}_done", 2, "act") for l in range(2)]
        pT_s = [count(f"pT{l}_saved", 4, "act") for l in range(2)]
        oh_s = count("oh_saved", 1, "act")
        x1h_s = count("x1h_saved", 1, "act")
        hT_s = count("hopT_saved", 2 * NUM_HOP, "act")

        k_s = [count(f"k{l}_saved", 1, "dve") for l in range(2)]
        v_s = [count(f"v{l}_saved", 1, "dve") for l in range(2)]
        mx = [count(f"masked{l}_done", 4, "dve") for l in range(2)]
        prd_s = count("probs1_last_done", 1, "dve")
        rec_s = [count(f"rec{l}_done", 2, "dve") for l in range(2)]
        tmp_s = count("rec1_raw_done", 2, "dve")
        xh_s = count("xh_saved", 1, "dve")
        xl_s = count("xl_saved", 1, "dve")
        mask_s = count("mask_done", 1, "dve")
        ol_s = count("ol_saved", 1, "dve")
        y_s = count("y0_saved", 1, "dve")
        bn_s = [count(f"bn{l}_done", 1, "dve") for l in range(2)]
        ag_s = [count(f"aggr{l}_done", 1, "dve") for l in range(2)]
        ve_s = [count(f"var_eps{l}_done", 1, "dve") for l in range(2)]
        yg_s = [count(f"centred{l}_done", 1, "dve") for l in range(2)]
        x1_s = count("x1_done", 1, "dve")
        o_s = count("out_done", 1, "dve")
        x1l_s = count("x1l_saved", 1, "dve")
        z_s = count("hop_saved", 2 * NUM_HOP, "dve")

        xb_s = count("xb_done", 1, "pool")
        pr_s = [count(f"probs{l}_done", 2, "pool") for l in range(2)]
        rstd_s = [count(f"rstd{l}_done", 1, "pool") for l in range(2)]
        z0_s = count("z0s_done", 1, "pool")
        zf_s = count("zf_done", 1, "pool")

        in_s = DmaCount([sem("in_even"), sem("in_odd")], 3)
        st_s = DmaCount([sem("store_even"), sem("store_odd")], 1)
        w_in = [sem(f"w_in{i}") for i in range(NW)]
        c_in = sem("const_in")
        wh_s = sem("w_hi_done")
        wl_s = sem("w_lo_done")
        bq_s = sem("bq0s_done")
        mh_s = sem("mhalf_done")
        xt_first = sem("first_xT_in")
        col_in = sem("column_biases_in")
        last_hr = [sem(f"last_hopT{b}_ready") for b in range(2)]
        last_hT = [sem(f"last_hopT{b}_saved") for b in range(2)]
        last_zr = [sem(f"last_hop{b}_ready") for b in range(2)]
        last_z = [sem(f"last_hop{b}_saved") for b in range(2)]
        own = sem("own_instruction")

        block = ctx.enter_context(nc.Block())

        def credit(eng, who):
            for c in owned[who]:
                eng.sem_inc(c.sem, c.per * SPARE)

        def pipeline(eng, begin, step, end, front=0, back=0):
            begin()
            first, turns = 1 + 2 * front, (PAIRS - 2) // 2 - front - back
            for t in range(1, first):
                step(Pair(0, t))
            with eng.Fori(0, turns) as i:
                for u in range(2):
                    step(Pair(i, first + u))
            for t in range(first + 2 * turns, PAIRS - 1):
                step(Pair(0, t))
            end()

        def both(row_i):
            return row[:, row_i:row_i + 1, :].broadcast_to([128, 2, D])

        @block.sync
        def _(sp):
            for s in st_s.sems:
                sp.sem_inc(s, 16)
            for s in in_s.sems:
                sp.sem_inc(s, in_s.per)

            def load_xt(p, done):
                sp.dma_start(xt_in[p.parity][:, :, :], x_t[bass.ds(p.number, 1)].rearrange("a p c t -> (a p) c t")
                             ).then_inc(done, 16)

            def load_adj(p):
                sp.dma_start(adj_in[p.parity][:, :, :], adj[bass.ds(p.number * 2, 2)].rearrange("b n m -> n b m")
                             ).then_inc(in_s.sem(p), 16)

            def load_x(p):
                sp.dma_start(x_in[p.parity][:, :, :], x[bass.ds(p.number * 2, 2)].rearrange("b n d -> n b d")
                             ).then_inc(in_s.sem(p), 16)

            def load(p):
                sp.wait_ge(xl_s.sem, xl_s.at(p - 2))
                sp.wait_ge(xb_s.sem, xb_s.at(p - 2))
                sp.wait_ge(mask_s.sem, mask_s.at(p - 2))
                load_xt(p, in_s.sem(p))
                load_adj(p)
                load_x(p)

            def load_w(i):
                sp.dma_start(w_raw[:, i, :, :], w[i].rearrange("(c p) o -> p c o", p=128)).then_inc(w_in[i], 16)

            def store(p):
                sp.wait_ge(o_s.sem, o_s.at(p))
                sp.dma_start(out[bass.ds(p.number * 2, 2)].rearrange("b n d -> n b d"), o_t[p.parity][:, :, :]
                             ).then_inc(st_s.sem(p), 16)

            def begin():
                load_xt(P0, xt_first)
                sp.sem_inc(in_s.sem(P0), 16)
                load_w(0)
                load_w(1)
                sp.dma_start(col[:, :, :], cols).then_inc(col_in, 16)
                load_w(2)
                load_adj(P0)
                sp.dma_start(row[:, :, :], rows.partition_broadcast(128)).then_inc(c_in, 16)
                load(P1)
                sp.dma_start(ident[:, :], ident_d).then_inc(c_in, 16)
                load_w(3)
                load_x(P0)
                for i in range(4, NW):
                    load_w(i)
                load(P0 + 2)

            def step(t):
                if not isinstance(t.i, int) or t.c + 2 < PAIRS:
                    load(t + 2)
                store(t - 1)

            def end():
                store(Q)
                store(R)

            pipeline(sp, begin, step, end, back=1)
            for p in (Q, R):
                sp.wait_ge(st_s.sem(p), st_s.at(p))

        @block.tensor
        def _(pe):
            credit(pe, "pe")
            parts = ((0, 0), (0, 1), (1, 0))

            def project_T(l, wi, c, dst, done, low=None):
                x_p, w_p = (xh[l], xl[l]), (w_hi, w_lo)
                for n, (a, e) in enumerate(parts):
                    if a and low:
                        pe.wait_ge(*low)
                    for kc in range(C):
                        last = nc.tensor.matmul(dst[:, c * T:(c + 1) * T], w_p[e][:, wi, kc, c * 128:(c + 1) * 128],
                                                x_p[a][:, kc, :], start=(n == 0 and kc == 0),
                                                stop=(n == 2 and kc == C - 1))
                if c == C - 1:
                    last.then_inc(done.sem, 1)

            def project(x_p, b, wi, dst, done, low=None):
                w_p = (w_hi, w_lo)
                for n, (a, e) in enumerate(parts):
                    if a and low:
                        pe.wait_ge(*low)
                    for kc in range(C):
                        last = nc.tensor.matmul(dst[:, b * D:(b + 1) * D], x_p[a](kc), w_p[e][:, wi, kc, :],
                                                start=(n == 0 and kc == 0), stop=(n == 2 and kc == C - 1))
                if b:
                    last.then_inc(done.sem, 1)

            def values(l, b, dst):
                project([lambda kc, m=m: m[:, kc, b * N:(b + 1) * N] for m in (xh[l], xl[l])], b,
                        (2, 6)[l], dst, vr[l])

            def scores(l, b, c):
                for g in range(G):
                    r = slice(32 * g, 32 * g + 32)
                    o = 512 * g + (b * C + c) * N
                    last = nc.tensor.matmul(psS[:, o:o + N], qT[l][r, c, b * N:(b + 1) * N],
                                            kT[l][r, c, b * N:(b + 1) * N], start=True, stop=True)
                if b and c == C - 1:
                    last.then_inc(sr[l].sem, 1)

            def turn_x1(p):
                pe.wait_ge(x1_s.sem, x1_s.at(p))
                for kc in range(C):
                    for b in range(2):
                        o = kc * T + b * N
                        last = nc.tensor.transpose(psM[0][:, o:o + N], x1[p.parity][:, b, kc * 128:(kc + 1) * 128],
                                                   ident[:, :])
                last.then_inc(x1r.sem, 1)

            def output(p):
                pe.wait_ge(oh_s.sem, oh_s.at(p))
                for b in range(2):
                    project([lambda c, m=m: m[:, b * C + c, :] for m in (oh, ol)], b, 3, psT[0], wor,
                            low=(ol_s.sem, ol_s.at(p)) if b == 0 else None)

            def turn_probs(l, p, b, c):
                if c == 0:
                    pe.wait_ge(pr_s[l].sem, pr_s[l].at(p, b + 1))
                elif b and l:
                    pe.wait_ge(prd_s.sem, prd_s.at(p))
                if b:
                    pe.wait_ge(pT_s[l].sem, pT_s[l].at(p, c + 1))
                for g in range(G):
                    last = nc.tensor.transpose(turned[l][c][:, g * N:(g + 1) * N], pr[l][:, b, G * c + g, :],
                                               ident[:, :])
                last.then_inc(tr[l].sem, 1)

            def spread(l, b, src, dst, done):
                for c in range(C):
                    for g in range(G):
                        h, o = G * c + g, (b * C + c) * N
                        last = nc.tensor.matmul(dst[32 * g:32 * g + 32, o:o + N],
                                                src[:, b, h * HD:(h + 1) * HD], pT[l][:, b, h, :],
                                                start=True, stop=True)
                if b:
                    last.then_inc(done.sem, 1)

            def attend(p):
                pe.wait_ge(v_s[0].sem, v_s[0].at(p))
                for b in range(2):
                    pe.wait_ge(pT_s[0].sem, pT_s[0].at(p, 3 + b))
                    spread(0, b, v[0], psM[0], avr)

            def hop(p, j):
                for b in range(2):
                    if j:
                        pe.wait_ge(z_s.sem, z_s.at(p, 2 * j - 1 + b))
                    spread(1, b, z if j else v[1], psT[0], hr)

            def turn_hop(p, j):
                for b in range(2):
                    pe.wait_ge(hT_s.sem, hT_s.at(p, 2 * j + 1 + b))
                    for c in range(C):
                        o = b * D + c * 128
                        last = nc.tensor.transpose(psT[1][:, o:o + 128], hT[:, b, c, :], ident[:, :])
                last.then_inc(zr.sem, 1)

            def last_turn_probs(p):
                pe.wait_ge(mx[1].sem, mx[1].at(p))
                for b in range(2):
                    for c in range(C):
                        if c == 0:
                            pe.wait_ge(pr_s[1].sem, pr_s[1].at(p, b + 1))
                        elif b:
                            pe.wait_ge(prd_s.sem, prd_s.at(p))
                        for g in range(G):
                            o = 512 * (2 * b + c) + g * N
                            last = nc.tensor.transpose(psS[:, o:o + N], pr[1][:, b, G * c + g, :], ident[:, :])
                        last.then_inc(tr[1].sem, 1)

            def last_hops(p):
                for j in range(NUM_HOP):
                    for b in range(2):
                        if j:
                            pe.wait_ge(last_z[b], j)
                        else:
                            pe.wait_ge(pT_s[1].sem, pT_s[1].at(p, 2 * b + 2))
                        for c in range(C):
                            for g in range(G):
                                h = G * c + g
                                last = nc.tensor.matmul(last_hopT[b][32 * g:32 * g + 32, c * N:(c + 1) * N],
                                                        (z if j else v[1])[:, b, h * HD:(h + 1) * HD],
                                                        pT[1][:, b, h, :], start=True, stop=True)
                        last.then_inc(last_hr[b], 1)
                    for b in range(2):
                        pe.wait_ge(last_hT[b], j + 1)
                        for c in range(C):
                            last = nc.tensor.transpose(last_hop[b][:, c * 128:(c + 1) * 128], hT[:, b, c, :], ident[:, :])
                        last.then_inc(last_zr[b], 1)

            def begin():
                pe.wait_ge(xh_s.sem, xh_s.at(P0))
                for p in (P0, P1):
                    if p is P0:
                        pe.wait_ge(wh_s, 1)
                        pe.wait_ge(wl_s, 1)
                    pe.wait_ge(xl_s.sem, xl_s.at(p))
                    pe.wait_ge(q_s[0].sem, q_s[0].at(p - 1))
                    project_T(0, 0, 0, psM[1], qr[0])
                    project_T(0, 0, 1, psM[1], qr[0])
                    if p is P0:
                        pe.wait_ge(wh_s, 2)
                        pe.wait_ge(wl_s, 2)
                    pe.wait_ge(k_s[0].sem, k_s[0].at(p - 1))
                    project_T(0, 1, 0, psM[0], kr[0])
                    project_T(0, 1, 1, psM[0], kr[0])
                    if p is P0:
                        pe.wait_ge(wh_s, 3)
                        pe.wait_ge(wl_s, 3)
                    pe.wait_ge(v_s[0].sem, v_s[0].at(p - 1))
                    values(0, 0, psT[1])
                    values(0, 1, psT[1])
                    pe.wait_ge(q_s[0].sem, q_s[0].at(p))
                    pe.wait_ge(k_s[0].sem, k_s[0].at(p))
                    pe.wait_ge(mx[0].sem, mx[0].at(p - 1))
                    for b in range(2):
                        scores(0, b, 0)
                        scores(0, b, 1)
                pe.wait_ge(c_in, 32)
                for b in range(2):
                    turn_probs(0, P0, b, 0)
                    turn_probs(0, P0, b, 1)
                attend(P0)
                pe.wait_ge(wh_s, NW)
                pe.wait_ge(wl_s, NW)
                output(P0)
                pe.wait_ge(ol_s.sem, ol_s.at(P0))
                turn_probs(0, P1, 0, 0)
                pe.wait_ge(y_s.sem, y_s.at(P0))
                turn_probs(0, P1, 0, 1)
                turn_probs(0, P1, 1, 0)
                turn_probs(0, P1, 1, 1)
                pe.wait_ge(pT_s[0].sem, pT_s[0].at(P1, 3))
                turn_x1(P0)
                pe.wait_ge(x1h_s.sem, x1h_s.at(P0))
                project_T(1, 4, 0, psM[1], qr[1], low=(x1l_s.sem, x1l_s.at(P0)))
                project_T(1, 4, 1, psM[1], qr[1])
                project_T(1, 5, 0, psM[0], kr[1])
                project_T(1, 5, 1, psM[0], kr[1])
                pe.wait_ge(mx[0].sem, mx[0].at(P1))
                pe.wait_ge(q_s[1].sem, q_s[1].at(P0))
                values(1, 0, psM[1])
                pe.wait_ge(k_s[1].sem, k_s[1].at(P0))
                scores(1, 0, 0)
                scores(1, 0, 1)
                values(1, 1, psM[1])
                scores(1, 1, 0)
                scores(1, 1, 1)

            def step(t):
                p, n = t - 1, t + 1
                attend(t)
                pe.wait_ge(xl_s.sem, xl_s.at(n))
                pe.wait_ge(v_s[1].sem, v_s[1].at(p))
                project_T(0, 0, 0, psM[1], qr[0])
                project_T(0, 0, 1, psM[1], qr[0])
                output(t)
                project_T(0, 1, 0, psM[0], kr[0])
                project_T(0, 1, 1, psM[0], kr[0])
                pe.wait_ge(z_s.sem, z_s.at(p - 1))
                values(0, 0, psT[1])
                values(0, 1, psT[1])
                pe.wait_ge(q_s[0].sem, q_s[0].at(n))
                pe.wait_ge(k_s[0].sem, k_s[0].at(n))
                pe.wait_ge(mx[1].sem, mx[1].at(p))
                scores(0, 0, 0)
                scores(0, 0, 1)
                pe.wait_ge(y_s.sem, y_s.at(t))
                turn_probs(1, p, 0, 0)
                pe.wait_ge(v_s[0].sem, v_s[0].at(n))
                turn_probs(1, p, 0, 1)
                scores(0, 1, 0)
                turn_probs(1, p, 1, 0)
                turn_probs(1, p, 1, 1)
                turn_x1(t)
                scores(0, 1, 1)
                pe.wait_ge(pT_s[1].sem, pT_s[1].at(p))
                hop(p, 0)
                pe.wait_ge(x1h_s.sem, x1h_s.at(t))
                project_T(1, 4, 0, psM[1], qr[1], low=(x1l_s.sem, x1l_s.at(t)))
                turn_hop(p, 0)
                project_T(1, 4, 1, psM[1], qr[1])
                hop(p, 1)
                project_T(1, 5, 0, psM[0], kr[1])
                turn_hop(p, 1)
                project_T(1, 5, 1, psM[0], kr[1])
                hop(p, 2)
                pe.wait_ge(q_s[1].sem, q_s[1].at(t))
                values(1, 0, psM[1])
                turn_hop(p, 2)
                pe.wait_ge(k_s[1].sem, k_s[1].at(t))
                pe.wait_ge(mx[0].sem, mx[0].at(n))
                scores(1, 0, 0)
                hop(p, 3)
                scores(1, 0, 1)
                turn_hop(p, 3)
                scores(1, 1, 0)
                turn_probs(0, n, 0, 0)
                turn_probs(0, n, 0, 1)
                scores(1, 1, 1)
                turn_probs(0, n, 1, 0)
                turn_probs(0, n, 1, 1)
                values(1, 1, psM[1])

            def end():
                attend(R)
                output(R)
                turn_x1(R)
                pe.wait_ge(z_s.sem, z_s.at(Q - 1))
                pe.wait_ge(y_s.sem, y_s.at(R))
                for c in range(C):
                    turn_probs(1, Q, 0, c)
                pe.wait_ge(v_s[1].sem, v_s[1].at(Q))
                pe.wait_ge(x1h_s.sem, x1h_s.at(R))
                project_T(1, 4, 0, psM[1], qr[1], low=(x1l_s.sem, x1l_s.at(R)))
                project_T(1, 4, 1, psM[1], qr[1])
                for c in range(C):
                    turn_probs(1, Q, 1, c)
                project_T(1, 5, 0, psM[0], kr[1])
                project_T(1, 5, 1, psM[0], kr[1])
                pe.wait_ge(pT_s[1].sem, pT_s[1].at(Q))
                hop(Q, 0)
                pe.wait_ge(q_s[1].sem, q_s[1].at(R))
                pe.wait_ge(k_s[1].sem, k_s[1].at(R))
                pe.wait_ge(mx[1].sem, mx[1].at(Q))
                scores(1, 0, 0)
                scores(1, 0, 1)
                turn_hop(Q, 0)
                scores(1, 1, 0)
                scores(1, 1, 1)
                hop(Q, 1)
                values(1, 0, psM[1])
                turn_hop(Q, 1)
                hop(Q, 2)
                values(1, 1, psM[1])
                turn_hop(Q, 2)
                hop(Q, 3)
                turn_hop(Q, 3)
                last_turn_probs(R)
                pe.wait_ge(v_s[1].sem, v_s[1].at(R))
                pe.wait_ge(z_s.sem, z_s.at(Q))
                last_hops(R)

            pipeline(pe, begin, step, end)

        @block.scalar
        def _(act):
            credit(act, "act")
            def round_w(first, end):
                for i in range(first, end):
                    act.wait_ge(w_in[i], 16)
                    nc.scalar.activation(w_hi[:, i, :, :], w_raw[:, i, :, :], ACT.Copy).then_inc(wh_s, 1)

            round_w(0, 3)
            act.wait_ge(col_in, 16)
            act.wait_ge(bq_s, 1)

            def save_q(l, p, ps):
                act.wait_ge(qr[l].sem, qr[l].at(p))
                act.wait_ge(sr[l].sem, sr[l].at(p - 1))
                for c in range(C):
                    b = bq0s[:, c:c + 1] if l == 0 else col[:, 2, c:c + 1]
                    last = nc.scalar.activation(qT[l][:, c, :], ps[:, c * T:(c + 1) * T], ACT.Identity, bias=b,
                                                scale=SCALE if l == 0 else 1.0)
                last.then_inc(q_s[l].sem, 1)

            def exp_head(l, p, b, h):
                if h == 0:
                    act.wait_ge(pr_s[l].sem, pr_s[l].at(p - 1, b + 1))
                    if b and l:
                        act.wait_ge(prd_s.sem, prd_s.at(p - 1))
                if h % 4 == 0:
                    act.wait_ge(mx[l].sem, mx[l].at(p, 2 * b + h // 4 + 1))
                e = nc.scalar.activation(ex[l][:, b, h, :], sm[l][:, b, h, :], ACT.Exp, scale=-1.0,
                                         bias=nmax[l][:, b, h:h + 1], accum_out=tot[l][:, b, h:h + 1])
                if h == H - 1:
                    e.then_inc(exps[l].sem, 1)

            def save_pT(l, p, b, c):
                act.wait_ge(tr[l].sem, tr[l].at(p, 2 * b + c + 1))
                nc.scalar.activation(pT[l][:, b, G * c:G * c + G, :],
                                     turned[l][c][:, :].rearrange("p (g n) -> p g n", g=G), ACT.Copy
                                     ).then_inc(pT_s[l].sem, 1)

            def save_hop(p, j):
                act.wait_ge(hr.sem, hr.at(p, j + 1))
                if j:
                    act.wait_ge(zr.sem, zr.at(p, j))
                else:
                    act.wait_ge(zr.sem, zr.at(p - 1))
                for b in range(2):
                    nc.scalar.activation(hT[:, b, :, :], psT[0][:, b * D:(b + 1) * D].rearrange("p (c n) -> p c n", c=C),
                                         ACT.Copy).then_inc(hT_s.sem, 1)

            def exps_of(l, p, first, end):
                for k in range(first, end):
                    exp_head(l, p, k // H, k % H)

            def save_all_pT(l, p):
                users = hr if l else avr
                act.wait_ge(users.sem, users.at(p - 1))
                for b in range(2):
                    for c in range(C):
                        save_pT(l, p, b, c)

            def save_oh(p):
                act.wait_ge(avr.sem, avr.at(p))
                act.wait_ge(wor.sem, wor.at(p - 1))
                nc.scalar.activation(oh[:, :, :], psM[0][:, :].rearrange("p (a n) -> p a n", n=N), ACT.Copy
                                     ).then_inc(oh_s.sem, 1)

            def save_x1h(p):
                act.wait_ge(x1r.sem, x1r.at(p))
                act.wait_ge(vr[1].sem, vr[1].at(p - 1))
                nc.scalar.activation(xh[1][:, :, :], psM[0][:, :].rearrange("p (c t) -> p c t", c=C), ACT.Copy
                                     ).then_inc(x1h_s.sem, 1)

            def begin():
                save_q(0, P0, psM[1])
                round_w(3, NW)
                exps_of(0, P0, 0, 2)
                save_q(0, P1, psM[1])
                exps_of(0, P0, 2, 16)
                exps_of(0, P1, 0, 3)
                for c in range(C):
                    save_pT(0, P0, 0, c)
                exps_of(0, P1, 3, 5)
                for c in range(C):
                    save_pT(0, P0, 1, c)
                exps_of(0, P1, 5, 10)
                save_oh(P0)
                exps_of(0, P1, 10, 16)
                save_all_pT(0, P1)
                save_x1h(P0)
                save_q(1, P0, psM[1])

            def step(t):
                p, n = t - 1, t + 1
                exps_of(1, p, 0, 3)
                save_oh(t)
                exps_of(1, p, 3, 5)
                save_q(0, n, psM[1])
                exps_of(1, p, 5, 16)
                save_all_pT(1, p)
                save_x1h(t)
                save_hop(p, 0)
                exps_of(0, n, 0, 7)
                save_hop(p, 1)
                exps_of(0, n, 7, 8)
                save_q(1, t, psM[1])
                exps_of(0, n, 8, 11)
                save_hop(p, 2)
                exps_of(0, n, 11, 16)
                save_hop(p, 3)
                save_all_pT(0, n)

            def end():
                exps_of(1, Q, 0, 3)
                save_oh(R)
                exps_of(1, Q, 3, 16)
                save_x1h(R)
                act.wait_ge(hr.sem, hr.at(Q - 1))
                for c in range(C):
                    save_pT(1, Q, 0, c)
                save_q(1, R, psM[1])
                for c in range(C):
                    save_pT(1, Q, 1, c)
                save_hop(Q, 0)
                save_hop(Q, 1)
                exps_of(1, R, 0, 5)
                save_hop(Q, 2)
                exps_of(1, R, 5, 11)
                save_hop(Q, 3)
                exps_of(1, R, 11, 16)
                act.wait_ge(hr.sem, hr.at(Q))
                for b in range(2):
                    for c in range(C):
                        act.wait_ge(tr[1].sem, tr[1].at(R, 2 * b + c + 1))
                        o = 512 * (2 * b + c)
                        nc.scalar.activation(pT[1][:, b, G * c:G * c + G, :],
                                             psS[:, o:o + 512].rearrange("p (g n) -> p g n", g=G), ACT.Copy
                                             ).then_inc(pT_s[1].sem, 1)
                for j in range(NUM_HOP):
                    for b in range(2):
                        act.wait_ge(last_hr[b], j + 1)
                        if j:
                            act.wait_ge(last_zr[b], j)
                        else:
                            act.wait_ge(zr.sem, zr.at(Q))
                        nc.scalar.activation(hT[:, b, :, :], last_hopT[b][:, :C * N].rearrange("p (c n) -> p c n", c=C),
                                             ACT.Copy).then_inc(last_hT[b], 1)

            pipeline(act, begin, step, end)

        @block.vector
        def _(dve):
            credit(dve, "dve")
            def split_w(i):
                dve.wait_ge(wh_s, i + 1)
                nc.vector.tensor_tensor(w_lo[:, i, :, :], w_raw[:, i, :, :], w_hi[:, i, :, :].bitcast(FP32), ALU.subtract
                                        ).then_inc(wl_s, 1)

            def split_x(p):
                if p is P0:
                    dve.wait_ge(xt_first, 16)
                else:
                    dve.wait_ge(in_s.sem(p), in_s.at(p))
                dve.wait_ge(vr[0].sem, vr[0].at(p - 1))
                nc.vector.tensor_copy(xh[0][:, :, :], xt_in[p.parity][:, :, :]).then_inc(xh_s.sem, 1)
                dve.wait_ge(xh_s.sem, xh_s.at(p))
                nc.vector.tensor_tensor(xl[0][:, :, :], xt_in[p.parity][:, :, :], xh[0][:, :, :].bitcast(FP32),
                                        ALU.subtract).then_inc(xl_s.sem, 1)

            def make_mask(p):
                dve.wait_ge(in_s.sem(p), in_s.at(p))
                dve.wait_ge(mx[1].sem, mx[1].at(p - 2))
                nc.vector.tensor_scalar(mask[p.parity][:, :, :], adj_in[p.parity][:, :, :], 0.0, MASKED,
                                        ALU.is_equal, ALU.mult).then_inc(mask_s.sem, 1)

            def save_k(l, p, ps):
                dve.wait_ge(kr[l].sem, kr[l].at(p))
                dve.wait_ge(sr[l].sem, sr[l].at(p - 1))
                for c in range(C):
                    last = nc.vector.tensor_scalar(kT[l][:, c, :], ps[:, c * T:(c + 1) * T],
                                                   col[:, 2 * l + 1, c:c + 1], None, ALU.add)
                last.then_inc(k_s[l].sem, 1)

            def save_v(l, p, ps):
                dve.wait_ge(vr[l].sem, vr[l].at(p))
                if l == 0:
                    dve.wait_ge(avr.sem, avr.at(p - 1))
                else:
                    dve.wait_ge(hr.sem, hr.at(p - 1, 1))
                    dve.wait_ge(z0_s.sem, z0_s.at(p - 1))
                nc.vector.tensor_tensor(v[l][:, :, :], ps[:, :].rearrange("p (b d) -> p b d", b=2),
                                        both(BV1 if l else BV0), ALU.add).then_inc(v_s[l].sem, 1)

            def mask_scores(l, p, b, c):
                if b == 0 and c == 0:
                    dve.wait_ge(sr[l].sem, sr[l].at(p))
                    dve.wait_ge(mask_s.sem, mask_s.at(p))
                    dve.wait_ge(exps[l].sem, exps[l].at(p - 1))
                    dve.sem_inc(own, 1)
                for g in range(G):
                    h, o = G * c + g, 512 * g + (b * C + c) * N
                    last = nc.vector.tensor_tensor_reduce(
                        sm[l][:, b, h, :], psS[:, o:o + N], mask[p.parity][:, b, :], -1.0, BIG,
                        ALU.add, ALU.min, nmax[l][:, b, h:h + 1])
                last.then_inc(mx[l].sem, 1)

            def reciprocals(l, p, b):
                dve.wait_ge(exps[l].sem, exps[l].at(p, b + 1))
                dve.wait_ge(pr_s[l].sem, pr_s[l].at(p - 1, b + 1))
                r = nc.vector.reciprocal(rec[l][:, b, :], tot[l][:, b, :])
                if l:
                    r.then_inc(tmp_s.sem, 1)
                    dve.wait_ge(tmp_s.sem, tmp_s.at(p, b + 1))
                    r = nc.vector.tensor_scalar(rec[l][:, b, :], rec[l][:, b, :], 1.0 - ALPHA, None, ALU.mult)
                r.then_inc(rec_s[l].sem, 1)

            def statistics(l, p):
                for b in range(2):
                    last = nc.vector.bn_stats(bst[l][:, b, :], y[l][:, b, :])
                last.then_inc(bn_s[l].sem, 1)

            def aggregate(l, p):
                dve.wait_ge(bn_s[l].sem, bn_s[l].at(p))
                dve.sem_inc(own, 1)
                for b in range(2):
                    last = nc.vector.bn_aggr(mv[l][:, b, :], bst[l][:, b, :])
                last.then_inc(ag_s[l].sem, 1)
                dve.wait_ge(ag_s[l].sem, ag_s[l].at(p))
                dve.wait_ge(rstd_s[l].sem, rstd_s[l].at(p - 1))
                nc.vector.tensor_scalar(ve[l][:, :], mv[l][:, :, 1], LN_EPS, None, ALU.add).then_inc(ve_s[l].sem, 1)

            def centre(l, p):
                for b in range(2):
                    last = nc.vector.scalar_tensor_tensor(out=yg[l][:, b, :], in0=y[l][:, b, :], scalar=mv[l][:, b, 0:1],
                                                          in1=row[:, GA1 if l else GA0, :], op0=ALU.subtract, op1=ALU.mult)
                last.then_inc(yg_s[l].sem, 1)

            def scale(l, p):
                dve.wait_ge(rstd_s[l].sem, rstd_s[l].at(p))
                dve.wait_ge(yg_s[l].sem, yg_s[l].at(p))
                if l:
                    dve.wait_ge(st_s.sem(p), st_s.at(p - 2))
                    dst, done = o_t[p.parity], o_s
                else:
                    dve.wait_ge(x1r.sem, x1r.at(p - 2))
                    dve.wait_ge(zf_s.sem, zf_s.at(p - 2))
                    dst, done = x1[p.parity], x1_s
                for b in range(2):
                    last = nc.vector.scalar_tensor_tensor(out=dst[:, b, :], in0=yg[l][:, b, :], scalar=rstd[l][:, b:b + 1],
                                                          in1=row[:, BE1 if l else BE0, :], op0=ALU.mult, op1=ALU.add)
                last.then_inc(done.sem, 1)

            def add_hop(p, j):
                dve.wait_ge(zr.sem, zr.at(p, j + 1))
                end = j == NUM_HOP - 1
                for b in range(2):
                    nc.vector.tensor_tensor((y[1] if end else z)[:, b, :], psT[1][:, b * D:(b + 1) * D],
                                            (zf if end else z0s)[:, b, :], ALU.add).then_inc(z_s.sem, 1)

            def save_ol(p):
                dve.wait_ge(oh_s.sem, oh_s.at(p))
                dve.wait_ge(wor.sem, wor.at(p - 1))
                nc.vector.tensor_tensor(ol[:, :, :], psM[0][:, :].rearrange("p (a n) -> p a n", n=N),
                                        oh[:, :, :].bitcast(FP32), ALU.subtract).then_inc(ol_s.sem, 1)

            def save_x1l(p):
                dve.wait_ge(x1h_s.sem, x1h_s.at(p))
                nc.vector.tensor_tensor(xl[1][:, :, :], psM[0][:, :].rearrange("p (c t) -> p c t", c=C),
                                        xh[1][:, :, :].bitcast(FP32), ALU.subtract).then_inc(x1l_s.sem, 1)

            def save_y(p):
                dve.wait_ge(wor.sem, wor.at(p))
                dve.wait_ge(xb_s.sem, xb_s.at(p))
                nc.vector.tensor_tensor(y[0][:, :, :], psT[0][:, :].rearrange("p (b d) -> p b d", b=2), xb[:, :, :],
                                        ALU.add).then_inc(y_s.sem, 1)

            def last_probabilities(p):
                dve.wait_ge(rec_s[1].sem, rec_s[1].at(p))
                dve.wait_ge(tr[1].sem, tr[1].at(p - 1))
                nc.vector.tensor_tensor(pr[1][:, 1, G:, :], ex[1][:, 1, G:, :],
                                        rec[1][:, 1, G:].unsqueeze(2).broadcast_to([128, G, N]), ALU.mult
                                        ).then_inc(prd_s.sem, 1)

            def mask_all(l, p):
                for b in range(2):
                    mask_scores(l, p, b, 0)
                    mask_scores(l, p, b, 1)

            def begin():
                split_x(P0)
                dve.wait_ge(col_in, 16)
                split_w(0)
                nc.vector.tensor_scalar(bq0s[:, :], col[:, 0, :], SCALE, None, ALU.mult).then_inc(bq_s, 1)
                split_w(1)
                split_w(2)
                save_k(0, P0, psM[0])
                split_x(P1)
                dve.wait_ge(c_in, 32)
                save_v(0, P0, psT[1])
                make_mask(P0)
                mask_all(0, P0)
                save_k(0, P1, psM[0])
                make_mask(P1)
                for i in range(3, NW):
                    split_w(i)
                reciprocals(0, P0, 0)
                reciprocals(0, P0, 1)
                mask_all(0, P1)
                save_ol(P0)
                save_v(0, P1, psT[1])
                reciprocals(0, P1, 0)
                reciprocals(0, P1, 1)
                save_y(P0)
                dve.wait_ge(y_s.sem, y_s.at(P0))
                statistics(0, P0)
                aggregate(0, P0)
                centre(0, P0)
                scale(0, P0)
                split_x(P0 + 2)
                save_x1l(P0)
                save_k(1, P0, psM[0])
                save_v(1, P0, psM[1])
                mask_scores(1, P0, 0, 0)
                mask_scores(1, P0, 0, 1)

            def step(t):
                p, n = t - 1, t + 1
                save_ol(t)
                mask_scores(1, p, 1, 0)
                mask_scores(1, p, 1, 1)
                save_y(t)
                reciprocals(1, p, 0)
                save_k(0, n, psM[0])
                dve.wait_ge(y_s.sem, y_s.at(t))
                statistics(0, t)
                save_v(0, n, psT[1])
                aggregate(0, t)
                reciprocals(1, p, 1)
                centre(0, t)
                last_probabilities(p)
                scale(0, t)
                if not (isinstance(t.i, int) and t.c == 1):
                    centre(1, p - 1)
                    scale(1, p - 1)
                make_mask(n)
                save_x1l(t)
                mask_scores(0, n, 0, 0)
                mask_scores(0, n, 0, 1)
                dve.wait_ge(zf_s.sem, zf_s.at(p))
                add_hop(p, 0)
                mask_scores(0, n, 1, 0)
                mask_scores(0, n, 1, 1)
                add_hop(p, 1)
                if not (isinstance(t.i, int) and t.c + 2 >= PAIRS):
                    split_x(t + 2)
                reciprocals(0, n, 0)
                save_k(1, t, psM[0])
                add_hop(p, 2)
                reciprocals(0, n, 1)
                add_hop(p, 3)
                dve.wait_ge(z_s.sem, z_s.at(p))
                statistics(1, p)
                aggregate(1, p)
                mask_scores(1, t, 0, 0)
                mask_scores(1, t, 0, 1)
                save_v(1, t, psM[1])

            def end():
                save_ol(R)
                mask_scores(1, Q, 1, 0)
                mask_scores(1, Q, 1, 1)
                save_y(R)
                dve.wait_ge(y_s.sem, y_s.at(R))
                statistics(0, R)
                reciprocals(1, Q, 0)
                aggregate(0, R)
                centre(0, R)
                scale(0, R)
                reciprocals(1, Q, 1)
                last_probabilities(Q)
                save_x1l(R)
                centre(1, Q - 1)
                scale(1, Q - 1)
                save_k(1, R, psM[0])
                dve.wait_ge(zf_s.sem, zf_s.at(Q))
                add_hop(Q, 0)
                mask_scores(1, R, 0, 0)
                mask_scores(1, R, 0, 1)
                add_hop(Q, 1)
                mask_scores(1, R, 1, 0)
                mask_scores(1, R, 1, 1)
                add_hop(Q, 2)
                reciprocals(1, R, 0)
                add_hop(Q, 3)
                save_v(1, R, psM[1])
                reciprocals(1, R, 1)
                last_probabilities(R)
                dve.wait_ge(z_s.sem, z_s.at(Q))
                statistics(1, Q)
                aggregate(1, Q)
                centre(1, Q)
                for j in range(NUM_HOP):
                    last = j == NUM_HOP - 1
                    if j == 0:
                        dve.wait_ge(z0_s.sem, z0_s.at(R))
                    if j == 1:
                        scale(1, Q)
                    if last:
                        dve.wait_ge(zf_s.sem, zf_s.at(R))
                    for b in range(2):
                        dve.wait_ge(last_zr[b], j + 1)
                        nc.vector.tensor_tensor((y[1] if last else z)[:, b, :], last_hop[b][:, :D],
                                                (zf if last else z0s)[:, b, :], ALU.add).then_inc(last_z[b], 1)
                for b in range(2):
                    dve.wait_ge(last_z[b], NUM_HOP)
                statistics(1, R)
                aggregate(1, R)
                centre(1, R)
                scale(1, R)

            pipeline(dve, begin, step, end, front=1, back=1)

        @block.gpsimd
        def _(pool):
            credit(pool, "pool")
            nc.gpsimd.memset(mhalf[:, :], -0.5).then_inc(mh_s, 1)
            pool.wait_ge(mh_s, 1)
            pool.wait_ge(c_in, 32)

            def probabilities(l, p, b):
                heads = G if l and b else H
                pool.wait_ge(rec_s[l].sem, rec_s[l].at(p, b + 1))
                pool.wait_ge(tr[l].sem, tr[l].at(p - 1, 2 * b + 2))
                nc.gpsimd.tensor_tensor(pr[l][:, b, :heads, :], ex[l][:, b, :heads, :],
                                        rec[l][:, b, :heads].unsqueeze(2).broadcast_to([128, heads, N]), ALU.mult
                                        ).then_inc(pr_s[l].sem, 1)

            def inverse_root(l, p):
                pool.wait_ge(ve_s[l].sem, ve_s[l].at(p))
                pool.wait_ge((o_s if l else x1_s).sem, (o_s if l else x1_s).at(p - 1))
                nc.gpsimd.tensor_tensor(rstd[l][:, :], ve[l][:, :], mhalf[:, :], ALU.pow).then_inc(rstd_s[l].sem, 1)

            def add_bias(p):
                pool.wait_ge(in_s.sem(p), in_s.at(p))
                pool.wait_ge(y_s.sem, y_s.at(p - 1))
                nc.gpsimd.tensor_tensor(xb[:, :, :], x_in[p.parity][:, :, :], both(BO0), ALU.add
                                        ).then_inc(xb_s.sem, 1)

            def restart_terms(p):
                pool.wait_ge(v_s[1].sem, v_s[1].at(p))
                pool.wait_ge(z_s.sem, z_s.at(p - 1))
                pool.sem_inc(own, 1)
                nc.gpsimd.tensor_scalar(z0s[:, :, :], v[1][:, :, :], ALPHA, 0.0, ALU.mult, ALU.add
                                        ).then_inc(z0_s.sem, 1)
                pool.wait_ge(z0_s.sem, z0_s.at(p))
                pool.wait_ge(x1_s.sem, x1_s.at(p))
                nc.gpsimd.tensor_tensor(zf[:, :, :], z0s[:, :, :], x1[p.parity][:, :, :], ALU.add
                                        ).then_inc(zf_s.sem, 1)

            def begin():
                probabilities(0, P0, 0)
                probabilities(0, P0, 1)
                add_bias(P0)
                probabilities(0, P1, 0)
                probabilities(0, P1, 1)
                inverse_root(0, P0)

            def step(t):
                p, n = t - 1, t + 1
                add_bias(t)
                restart_terms(p)
                probabilities(1, p, 0)
                inverse_root(0, t)
                probabilities(1, p, 1)
                probabilities(0, n, 0)
                probabilities(0, n, 1)
                inverse_root(1, p)

            def end():
                add_bias(R)
                restart_terms(Q)
                inverse_root(0, R)
                probabilities(1, Q, 0)
                probabilities(1, Q, 1)
                probabilities(1, R, 0)
                probabilities(1, R, 1)
                restart_terms(R)
                inverse_root(1, Q)
                inverse_root(1, R)

            pipeline(pool, begin, step, end)


def kernel(**inputs):
    from concourse import bacc
    from concourse.bass_utils import run_bass_kernel_spmd

    def arr(name):
        return np.ascontiguousarray(inputs[name])

    x = arr("x")
    x_t = np.ascontiguousarray(x.reshape(PAIRS, T, C, 128).transpose(0, 3, 2, 1))
    w = np.stack([arr("L0_gnn_Wq"), arr("L0_gnn_Wk"), arr("L0_gnn_Wv"), arr("L0_gnn_Wo"),
                  arr("L1_gnn_Wq").T, arr("L1_gnn_Wk").T, arr("L1_gnn_Wv").T])
    rows = np.stack([arr(n) for n in ("L0_gnn_bv", "L0_gnn_bo", "L0_gnn_gamma", "L0_gnn_beta",
                                      "L1_gnn_bv", "L1_gnn_gamma", "L1_gnn_beta")])
    cols = np.ascontiguousarray(np.stack([arr(n).reshape(C, 128) for n in (
        "L0_gnn_bq", "L0_gnn_bk", "L1_gnn_bq", "L1_gnn_bk")]).transpose(2, 0, 1))
    ident = np.eye(128, dtype=np.float32)
    arrays = {"in_x": x, "in_x_t": x_t, "in_adj": arr("adj"), "in_w": w, "in_rows": rows, "in_cols": cols,
              "in_ident": ident}

    nc = bacc.Bacc("TRN2", target_bir_lowering=False, num_devices=1)
    aps = [nc.dram_tensor(k, a.shape, mybir.dt.from_np(a.dtype), kind="ExternalInput").ap()
           for k, a in arrays.items()]
    out = nc.dram_tensor("out", (B, N, D), FP32, kind="ExternalOutput").ap()
    two_layers(nc, *aps, out)
    r = run_bass_kernel_spmd(nc, [arrays], core_ids=[0])
    return r.results[0]["out"]
```
